# Optimizing a Trainium2 kernel written in Bass

```python
import numpy as np
import jax
import jax.numpy as jnp

def _softmax(x, axis=-1):
    return jax.nn.softmax(x, axis=axis)

def _gelu(x):
    return jax.nn.gelu(x, approximate=True)

def _silu(x):
    return jax.nn.silu(x)

def _sigmoid(x):
    return jax.nn.sigmoid(x)

def _layernorm(x, axis=-1, eps=1e-05):
    m = jnp.mean(x, axis=axis, keepdims=True)
    v = jnp.var(x, axis=axis, keepdims=True)
    return (x - m) / jnp.sqrt(v + eps)

def _scatter_add(tgt, idx, src, axis=0):
    return tgt.at[idx].add(src)

def _segment_sum(src, seg, n):
    return jax.ops.segment_sum(src, seg, n)
kernel_name = 'mk_adj_ffn_d1_adj_r2_957d17'

def setup_inputs(seed: int=0):
    np.random.seed(seed)
    _w = jnp.asarray

    def _rec_inputs():
        import jax
        import jax.numpy as jnp
        _gk = jax.random.key(seed)
        x = -0.0002928 + 1 * jax.random.normal(jax.random.fold_in(_gk, 1), (4096, 256), jnp.float32)
        _a = jax.random.bernoulli(jax.random.fold_in(_gk, 2), 0.000488281, (4096, 4096))
        _a = jnp.logical_or(_a, jnp.swapaxes(_a, -1, -2))
        _a = jnp.logical_or(_a, jnp.eye(4096, dtype=bool))
        _af = _a.astype(jnp.float32)
        _af = _af * jax.random.uniform(jax.random.fold_in(_gk, 3), (4096, 4096), jnp.float32, 0.05, 5.41998)
        adj = _af
        return (x, adj)
    x, adj = _rec_inputs()

    def _L0_gnn_setup():
        import jax, jax.numpy as jnp
        import numpy as np
        N = 4096
        D = 256
        EPS = 1e-12
        key = jax.random.key(seed)
        k1, k2 = jax.random.split(key)
        cur = jax.random.normal(k1, (N, D), dtype=jnp.float32)
        incidence_m = jax.random.normal(k2, (N, N), dtype=jnp.float32)
        return {'cur': cur, 'incidence_m': incidence_m}
    _L0_gnn_all = _L0_gnn_setup()
    _L0_gnn_in = {k: v for k, v in _L0_gnn_all.items() if k in ()}
    del _L0_gnn_all

    def _L0_ffn_setup():
        import jax, jax.numpy as jnp
        import numpy as np
        D_MODEL = 256
        DFF = 1024
        E = 8
        K = 2
        B, N = (2, 1024)
        key = jax.random.key(seed)
        ks = jax.random.split(key, 6)
        x = jax.random.normal(ks[0], (B, N, D_MODEL), dtype=jnp.float32)
        router_w = jax.random.normal(ks[1], (E, D_MODEL), dtype=jnp.float32) * 0.01
        lim1 = float(np.sqrt(6.0 / (D_MODEL + DFF)))
        w1_all = jax.random.uniform(ks[2], (E, DFF, D_MODEL), minval=-lim1, maxval=lim1, dtype=jnp.float32)
        w2_all = jax.random.uniform(ks[3], (E, D_MODEL, DFF), minval=-lim1, maxval=lim1, dtype=jnp.float32)
        b1_all = jax.random.normal(ks[4], (E, DFF), dtype=jnp.float32) * 0.01
        b2_all = jax.random.normal(ks[5], (E, D_MODEL), dtype=jnp.float32) * 0.01
        return {'x': x, 'router_w': router_w, 'w1_all': w1_all, 'b1_all': b1_all, 'w2_all': w2_all, 'b2_all': b2_all}
    _L0_ffn_all = _L0_ffn_setup()
    _L0_ffn_in = {k: v for k, v in _L0_ffn_all.items() if k in ('router_w', 'w1_all', 'b1_all', 'w2_all', 'b2_all')}
    del _L0_ffn_all
    return {'x': x, 'adj': adj, 'L0_ffn_router_w': _L0_ffn_in['router_w'], 'L0_ffn_w1_all': _L0_ffn_in['w1_all'], 'L0_ffn_b1_all': _L0_ffn_in['b1_all'], 'L0_ffn_w2_all': _L0_ffn_in['w2_all'], 'L0_ffn_b2_all': _L0_ffn_in['b2_all']}

def reference(x, adj, L0_ffn_router_w, L0_ffn_w1_all, L0_ffn_b1_all, L0_ffn_w2_all, L0_ffn_b2_all):
    import jax
    import jax.numpy as jnp

    def _L0_gnn_ref(cur, incidence_m):
        import jax, jax.numpy as jnp
        import numpy as np
        N = 4096
        D = 256
        EPS = 1e-12
        mask = incidence_m > 0
        head = jax.lax.stop_gradient(mask.astype(incidence_m.dtype))
        head = head / jnp.maximum(jnp.sqrt(jnp.sum(head * head, axis=-1, keepdims=True)), EPS)
        inc = incidence_m + head
        edge_fea = inc @ cur
        edge_degree = jnp.sum(inc, axis=-1, keepdims=True)
        return edge_fea / edge_degree

    def _L0_ffn_ref(x, router_w, w1_all, b1_all, w2_all, b2_all):
        import jax, jax.numpy as jnp
        import numpy as np
        D_MODEL = 256
        DFF = 1024
        E = 8
        K = 2
        B, N = (2, 1024)
        Bb, Nn, C = x.shape
        L = Bb * Nn
        x_flat = x.reshape(L, C)
        router_logits = x_flat @ router_w.T
        router_probs = jax.nn.softmax(router_logits, axis=-1)
        expert_weights, expert_indices = jax.lax.top_k(router_probs, K)
        expert_weights = expert_weights / (jnp.sum(expert_weights, axis=-1, keepdims=True) + 1e-09)
        h = jax.nn.relu(jnp.einsum('lc,efc->lef', x_flat, w1_all) + b1_all[None])
        out_all = jnp.einsum('lef,ecf->lec', h, w2_all) + b2_all[None]
        out_sel = jnp.take_along_axis(out_all, expert_indices[:, :, None], axis=1)
        final = jnp.sum(out_sel * expert_weights[:, :, None], axis=1)
        return final.reshape(Bb, Nn, C)
    x = x + _L0_gnn_ref(_layernorm(x, axis=-1), adj)
    x = x + _L0_ffn_ref(_layernorm(x, axis=-1)[None], L0_ffn_router_w, L0_ffn_w1_all, L0_ffn_b1_all, L0_ffn_w2_all, L0_ffn_b2_all)[0]
    return x

_drawn_inputs = setup_inputs


def setup_inputs(seed=0):
    import zlib

    import numpy as np

    out = dict(_drawn_inputs(seed))
    spreads = {}
    factors = {'L0_ffn_b1_all': 8.0, 'L0_ffn_b2_all': 8.0}
    for name, (base, spread) in spreads.items():
        noise = np.random.default_rng([zlib.crc32(name.encode()), seed]).standard_normal(out[name].shape)
        drawn = base * np.exp(spread * noise) if base else spread * noise
        out[name] = jnp.asarray(drawn.astype(out[name].dtype))
    for name, factor in factors.items():
        out[name] = (out[name] * factor).astype(out[name].dtype)
    return out
```

```python
from contextlib import ExitStack

import concourse.bass as bass
from concourse import mybir

P = 128
F32 = mybir.dt.float32
F16 = mybir.dt.float16
BF16 = mybir.dt.bfloat16
I32 = mybir.dt.int32
ALU = mybir.AluOpType
ACT = mybir.ActivationFunctionType
AX = mybir.AxisListType.X

N, D, DFF, E, K = 4096, 256, 1024, 8, 2
NT = N // P
NPAIR = NT // 2
UJ = NT // 2
UNIT = UJ * P
DC = D // P
FC = DFF // P
EPS = 1e-5
RSQRT_BITS = 0x5F3759DF
LNG = 4
LNT = NT // LNG

TT = 256
SUB = TT // P
TILES = (K * N + (TT - 1) * E) // TT
EROWS = N
ROWS = E * EROWS + (TILES - E) * TT
PADQ = ROWS // P
MATS = DC * DFF
EW = 4 * MATS
CH = MATS // 2
LAST = (TILES - 1) // 2
NC4 = 8
C4 = NT // NC4

SX = 264


def moe_gnn_kernel(nc, x, adj_u, w_all, b1_t, b2_r, rw_t, out):
    with ExitStack() as ctx:
        def sb(name, shape, dt=F32):
            return ctx.enter_context(nc.sbuf_tensor(name, shape, dt))

        def sem(name):
            return ctx.enter_context(nc.semaphore(name))

        def dram(name, shape, dt=F32):
            return nc.dram_tensor(name, shape, dt).ap()

        w_split = dram("w_split", (P, E, EW), F16)
        xn_rows = dram("xn_rows", (N + P, D))
        x1_rows = dram("x1_rows", (N, D))
        table = dram("table", (ROWS, 1), I32)
        y_rows = dram("y_rows", (K * N, D))

        W = sb("W", [P, E, EW], F16)
        Wf = W[:, :, :].rearrange("p e n -> p (e n)")
        lower = Wf[:, 0:4 * EW]
        upper = Wf[:, 4 * EW:8 * EW]
        xall = lower[:, 0:2 * NT * D].bitcast(F32).rearrange("p (t d) -> p t d", t=NT)
        adj_sb = upper[:, 0:4 * 2 * UNIT].bitcast(F32).rearrange("p (k n) -> p k n", k=4)
        at = 4 * 2 * UNIT
        parts = []
        for _ in range(6):
            parts.append(upper[:, at:at + UNIT])
            at += UNIT
        high, low, mask = parts[0:2], parts[2:4], parts[4:6]
        mask = [m.bitcast(BF16) for m in mask]
        y_sb = Wf[:, 0:32768].bitcast(F32).rearrange("p (t n) -> p t n", t=NT)
        x1_sb = Wf[:, 32768:49152].bitcast(F32).rearrange("p (t n) -> p t n", t=NT)
        o_sb = Wf[:, 49152:65536].bitcast(F32).rearrange("p (t n) -> p t n", t=NT)

        R = sb("R", [P, NT * SX + NT * D], F16)
        ch = R[:, 0:NT * SX].rearrange("p (t d) -> p t d", t=NT)
        cl = R[:, NT * SX:].rearrange("p (t d) -> p t d", t=NT)
        Rf = R[:, :]
        at = 0

        def region(n, dt):
            nonlocal at
            words = n if dt == F16 else 2 * n
            v = Rf[:, at:at + words]
            at += words
            return v if dt == F16 else v.bitcast(dt)

        hh = [region(FC * TT, F16) for _ in range(2)]
        hl = [region(FC * TT, F16) for _ in range(2)]
        h32 = region(FC * TT, F32)
        xg = [region(SUB * D, F32).rearrange("p (s d) -> p s d", s=SUB) for _ in range(2)]
        xh = [region(DC * TT, F16) for _ in range(2)]
        xl = [region(DC * TT, F16) for _ in range(2)]
        assert at <= NT * (SX + D)

        stage = sb("stage", [P, 2, CH])
        stage_h = sb("stage_h", [P, 2, CH], F16)
        stage_l = sb("stage_l", [P, 2, CH], F16)
        y_out = [stage[:, b, 0:SUB * D].rearrange("p (s d) -> p s d", s=SUB) for b in range(2)]
        b2 = sb("b2", [P, E, D])
        b1 = sb("b1", [P, E * FC])
        rw = sb("rw", [P, DC, E])
        xt = sb("xt", [P, 2, D])
        x1t = sb("x1t", [P, 2, D])
        xnt = sb("xnt", [P, 2, D])
        xnT = sb("xnT", [P, 2, D])
        wm = sb("wm", [P, 2, SX])
        num = sb("num", [P, 2, SX])
        zero = sb("zero", [P, D])
        ident = sb("ident", [P, P])
        tri = sb("tri", [P, P], BF16)
        ones = sb("ones", [P, P], BF16)
        stats = sb("stats", [P, NT, 6])
        mv = sb("mv", [P, NT, 2])
        rstd = sb("rstd", [P, NT])
        var = sb("var", [P, NT])
        newton = sb("newton", [P, NT])
        hscale = sb("hscale", [P, 2])
        rec = sb("rec", [P, 2])
        st2 = sb("st2", [P, 2, 6])
        mv2 = sb("mv2", [P, 2, 2])
        rs2 = sb("rs2", [P, 2])
        pad_codes = sb("pad_codes", [P, PADQ], I32)
        kv = sb("kv", [P, E])
        z = sb("z", [P, 2, E])
        ez = sb("ez", [P, 2, E])
        prob = sb("prob", [P, 2, E])
        prob2 = sb("prob2", [P, 2, E])
        eq = sb("eq", [P, 2, E])
        oh = sb("oh", [P, 2, 2, E])
        sel = sb("sel", [P, 2, E], BF16)
        mx = sb("mx", [P, 2])
        m1 = sb("m1", [P, 2])
        m2 = sb("m2", [P, 2])
        km = sb("km", [P, 2])
        sm = sb("sm", [P, 2])
        gates = sb("gates", [P, NT, K])
        count = sb("count", [P, E])
        pos = sb("pos", [P, 2, E])
        place = sb("place", [P, 2, 2, E])
        slots = sb("slots", [P, 2, 2], I32)
        codes = sb("codes", [P, 2, 2], I32)
        base = sb("base", [P, E])
        nt_i = sb("nt_i", [P, E], I32)
        nt_f = sb("nt_f", [P, E])
        end = sb("end", [P, E])
        jump = sb("jump", [P, E])
        ti = sb("ti", [1, TILES])
        past = sb("past", [1, TILES, E])
        pj = sb("pj", [1, TILES, E])
        te = sb("te", [1, TILES])
        tr = sb("tr", [1, TILES])
        tile_expert = sb("tile_expert", [1, TILES], I32)
        tile_row = sb("tile_row", [1, TILES], I32)
        tcodes = sb("tcodes", [P, TILES + 1, SUB], I32)
        tok = [sb(f"tok{b}", [P, SUB], I32) for b in range(2)]
        dest = [sb(f"dest{b}", [P, SUB], I32) for b in range(2)]

        PS = ctx.enter_context(nc.psum_tensor("PS", [P, 8, 512], F32))
        acc_adj = [PS[:, 0, :], PS[:, 1, :]]
        acc_mask = [PS[:, 2, :], PS[:, 3, :]]
        turned = [PS[:, 4, 0:D], PS[:, 5, 0:D]]
        logits = PS[:, 6, 0:2 * E].rearrange("p (u e) -> p u e", u=2)
        rank = PS[:, 7, 0:2 * E].rearrange("p (u e) -> p u e", u=2)
        total = PS[:, 7, 2 * E:3 * E]
        h1 = [PS[:, q, :] for q in range(4)]
        yp = [PS[:, 4, :], PS[:, 5, :]]
        xT = [PS[:, 6, :], PS[:, 7, :]]

        adj_in = [sem(f"adj_in{k}") for k in range(4)]
        x_all_in = [sem(f"x_all_in{g}") for g in range(LNG)]
        x_in = [sem(f"x_in{u}") for u in range(2)]
        small_in = sem("small_in")
        wf_in = [sem(f"wf_in{v}") for v in range(2)]
        wsplit_out = [sem(f"wsplit_out{v}") for v in range(2)]
        rows_out = [sem(f"rows_out{u}") for u in range(2)]
        pads_out = sem("pads_out")
        w_in = [sem(f"w_in{e}") for e in range(E)]
        code_put = sem("code_put")
        codes_in = [sem(f"codes_in{b}") for b in range(2)]
        xg_in = [sem(f"xg_in{b}") for b in range(2)]
        y_put = sem("y_put")
        yr_in = [sem(f"yr_in{b}") for b in range(2)]
        out_put = sem("out_put")
        consts = sem("consts")
        dconst = sem("dconst")
        ln_ready = sem("ln_ready")
        ch_ready = sem("ch_ready")
        cl_ready = sem("cl_ready")
        high_ready = sem("high_ready")
        mask_ready = sem("mask_ready")
        low_ready = sem("low_ready")
        unit_done = sem("unit_done")
        hscale_ready = sem("hscale_ready")
        wm_ready = sem("wm_ready")
        num_ready = sem("num_ready")
        xn_ready = sem("xn_ready")
        turn_ready = sem("turn_ready")
        xnT_ready = sem("xnT_ready")
        logits_ready = sem("logits_ready")
        z_ready = sem("z_ready")
        exp_ready = sem("exp_ready")
        sel_ready = sem("sel_ready")
        rank_ready = sem("rank_ready")
        slots_ready = sem("slots_ready")
        whigh_ready = sem("whigh_ready")
        wlow_ready = sem("wlow_ready")
        table_ready = sem("table_ready")
        tok_ready = sem("tok_ready")
        xt_ready = sem("xt_ready")
        xh_ready = sem("xh_ready")
        xl_ready = sem("xl_ready")
        h1_ready = sem("h1_ready")
        relu_ready = sem("relu_ready")
        hh_ready = sem("hh_ready")
        hl_ready = sem("hl_ready")
        yp_ready = sem("yp_ready")
        y_ready = sem("y_ready")
        dest_ready = sem("dest_ready")
        fin_part = sem("fin_part")
        fin_ready = sem("fin_ready")
        dve_step = sem("dve_step")
        act_step = sem("act_step")

        def wait(eng, s, value):
            if isinstance(value, int) and value <= 0:
                return
            eng.wait_ge(s, value)

        def waits_apart(eng, *pairs):
            pairs = [(s, v if isinstance(v, int) else eng.to_reg(v)) for s, v in pairs]
            if not all(isinstance(v, int) for _, v in pairs):
                eng.wait_ge(consts, 11)
            for s, v in pairs:
                wait(eng, s, v)

        def pairs(eng, body, tail):
            body(0)
            with eng.Fori(1, NPAIR) as i:
                body(i)
            tail(NPAIR)

        block = ctx.enter_context(nc.Block())

        @block.sync
        def _(sp):
            def load_unit(i, k):
                sp.dma_start(adj_sb[:, k, :],
                             adj_u[bass.ds(i, 1), k].rearrange("a p n -> p (a n)")).then_inc(adj_in[k], 16)

            def load_x(t, u):
                sp.dma_start(xt[:, u, :], x[bass.ds(t * P, P), :]).then_inc(x_in[u], 16)

            def load_w(c, v):
                sp.dma_start(stage[:, v, :], w_all[:, bass.ds(c * CH, CH)]).then_inc(wf_in[v], 16)

            def store_rows(t, u):
                wait(sp, xn_ready, t + 1)
                sp.dma_start(xn_rows[bass.ds(t * P, P), :], xnt[:, u, :]).then_inc(rows_out[u], 16)
                sp.dma_start(x1_rows[bass.ds(t * P, P), :], x1t[:, u, :]).then_inc(rows_out[u], 16)

            x_v = x.rearrange("(t p) d -> p t d", p=P)
            for g in range(LNG):
                sp.dma_start(xall[:, g * LNT:(g + 1) * LNT, :],
                             x_v[:, g * LNT:(g + 1) * LNT, :]).then_inc(x_all_in[g], 16)
                load_unit(0, g)
            sp.dma_start(rw[:, :, :], rw_t).then_inc(small_in, 16)
            sp.dma_start(b1[:, :], b1_t).then_inc(small_in, 16)
            sp.dma_start(b2[:, :, :], b2_r.to_broadcast([P, E, D])).then_inc(small_in, 16)
            for u in range(2):
                load_x(u, u)
                load_w(u, u)
            sp.wait_ge(dconst, 2)
            sp.dma_start(table.rearrange("(p q) o -> p (q o)", p=P), pad_codes[:, :]).then_inc(pads_out, 16)
            sp.dma_start(xn_rows[N:N + P, :], zero[:, :]).then_inc(pads_out, 16)

            def store_split(i, v):
                wait(sp, wlow_ready, 2 * i + v + 1)
                to = w_split.rearrange("p e (m h n) -> p (e m) h n", m=2, h=2)
                for h, part in enumerate((stage_h, stage_l)):
                    sp.dma_start(to[:, bass.ds(i, 1), h, v * CH:(v + 1) * CH].rearrange("p a n -> p (a n)"),
                                 part[:, v, :]).then_inc(wsplit_out[v], 16)

            def body(i, more=True):
                first = isinstance(i, int) and i == 0
                for k in range(4):
                    if more:
                        wait(sp, low_ready, 4 * i + k + 1)
                        load_unit(i + 1, k)
                    if k == 1 and not first:
                        store_rows(2 * i - 1, 1)
                        load_x(2 * i + 1, 1)
                    if k == 3:
                        store_rows(2 * i, 0)
                        if more:
                            load_x(2 * i + 2, 0)
                    if k in (1, 3):
                        store_split(i, k // 2)
                        if more:
                            load_w(2 * (i + 1) + k // 2, k // 2)

            body(0)
            with sp.Fori(1, NPAIR - 1) as i:
                body(i)
            body(NPAIR - 1, more=False)
            def load_codes(m, b):
                j = 2 * m + b
                row = sp.value_load(tile_row[0:1, bass.ds(j, 1)], min_val=0, max_val=ROWS - TT)
                wait(sp, codes_in[b], 16 * m)
                sp.dma_start(tcodes[:, bass.ds(j, 1), :].rearrange("p a s -> p (a s)"),
                             table[bass.ds(row, TT), :].rearrange("(p s) o -> p (s o)", s=SUB)
                             ).then_inc(codes_in[b], 16)

            for v in range(2):
                sp.wait_ge(wsplit_out[v], 32 * NPAIR)
            sp.wait_ge(cl_ready, LNG)
            for e in range(E):
                if e == 1:
                    store_rows(NT - 1, 1)
                if e == E // 2:
                    sp.wait_ge(unit_done, 2 * NT)
                sp.dma_start(W[:, e, :], w_split[:, e, :]).then_inc(w_in[e], 16)
                if e == E // 2:
                    sp.wait_ge(code_put, 16 * 4 * NPAIR)
                    sp.wait_ge(table_ready, 2)
                    load_codes(0, 0)
                    load_codes(0, 1)
            with sp.Fori(1, LAST) as m:
                load_codes(m, 0)
                load_codes(m, 1)
            load_codes(LAST, 0)

            sp.wait_ge(y_put, 16 * SUB * TILES)
            sp.wait_ge(yp_ready, TILES)
            for u in range(2):
                sp.wait_ge(rows_out[u], 32 * NPAIR)
            y_v = y_rows.rearrange("(t p k) d -> p t (k d)", p=P, k=K)
            x1_v = x1_rows.rearrange("(t p) d -> p t d", p=P)
            out_v = out.rearrange("(t p) d -> p t d", p=P)

            def load_rows(m, b):
                t = bass.ds((2 * m + b) * C4, C4)
                wait(sp, yr_in[b], 32 * m)
                sp.dma_start(y_sb[:, t, :], y_v[:, t, :]).then_inc(yr_in[b], 16)
                sp.dma_start(x1_sb[:, t, :], x1_v[:, t, :]).then_inc(yr_in[b], 16)

            with sp.Fori(0, NC4 // 2) as m:
                load_rows(m, 0)
                load_rows(m, 1)
            with sp.Fori(0, NC4) as c:
                wait(sp, fin_ready, C4 * (c + 1))
                t = bass.ds(c * C4, C4)
                sp.dma_start(out_v[:, t, :], o_sb[:, t, :]).then_inc(out_put, 16)
            sp.wait_ge(out_put, 16 * NC4)

        @block.gpsimd
        def _(pool):
            pool.memset(ident[:, :], 0.0).then_inc(consts, 1)
            pool.memset(tri[:, :], 1.0).then_inc(consts, 1)
            pool.memset(ones[:, :], 1.0).then_inc(consts, 1)
            pool.memset(ch[:, :, D:D + 2], 1.0).then_inc(consts, 1)
            pool.wait_ge(consts, 2)
            pool.affine_select(out=ident[:, :], in_=ident[:, :], compare_op=ALU.not_equal, fill=1.0,
                               base=0, pattern=[[-1, P]], channel_multiplier=1).then_inc(consts, 1)
            pool.affine_select(out=tri[:, :], in_=tri[:, :], compare_op=ALU.is_gt, fill=0.0,
                               base=0, pattern=[[1, P]], channel_multiplier=-1).then_inc(consts, 1)
            pool.iota(pad_codes[:, :], [[1, PADQ]], base=0, channel_multiplier=PADQ).then_inc(consts, 1)
            pool.iota(codes[:, :, :], [[1, 2], [2 * P, 2]], base=-4 * P, channel_multiplier=2).then_inc(consts, 1)
            pool.iota(kv[:, :], [[-1, E]], base=E, channel_multiplier=0,
                      allow_small_or_imprecise_dtypes=True).then_inc(consts, 1)
            pool.iota(base[:, :], [[EROWS, E]], base=0, channel_multiplier=0,
                      allow_small_or_imprecise_dtypes=True).then_inc(consts, 1)
            pool.iota(ti[:, :], [[1, TILES]], base=0, channel_multiplier=0,
                      allow_small_or_imprecise_dtypes=True).then_inc(consts, 1)

            for g in range(LNG):
                pool.wait_ge(ch_ready, g + 1)
                sl = slice(g * LNT, (g + 1) * LNT)
                pool.tensor_tensor(cl[:, sl, :], xall[:, sl, :], ch[:, sl, 0:D],
                                   ALU.subtract).then_inc(cl_ready, 1)

            def split(i, v):
                waits_apart(pool, (wf_in[v], 16 * (i + 1)), (wsplit_out[v], 32 * i))
                pool.tensor_copy(stage_h[:, v, :], stage[:, v, :]).then_inc(whigh_ready, 1)
                wait(pool, whigh_ready, 2 * i + v + 1)
                pool.tensor_tensor(stage_l[:, v, :], stage[:, v, :], stage_h[:, v, :],
                                   ALU.subtract).then_inc(wlow_ready, 1)

            def scatter(i):
                waits_apart(pool, (slots_ready, i + 1))
                for c in range(2):
                    for u in range(2):
                        n = 4 * i + 2 * c + u
                        waits_apart(pool, (code_put, 16 * n))
                        pool.indirect_dma_start(
                            table, bass.IndirectOffsetOnAxis(slots[:, c, u:u + 1], 0),
                            codes[:, c, u:u + 1], None).then_inc(code_put, 16)

            def body(i):
                split(i, 0)
                if not (isinstance(i, int) and i == 0):
                    scatter(i - 1)
                split(i, 1)

            pool.wait_ge(pads_out, 32)
            pairs(pool, body, lambda i: scatter(i - 1))

            def gather(m, b):
                j = 2 * m + b
                waits_apart(pool, (tok_ready, j + 1), (xt_ready, j - 1))
                if isinstance(j, int) and j < 2:
                    pool.wait_ge(rows_out[0], 32 * NPAIR)
                    pool.wait_ge(rows_out[1], 32 * NPAIR)
                for s in range(SUB):
                    pool.indirect_dma_start(xg[b][:, s, :], None, xn_rows,
                                            bass.IndirectOffsetOnAxis(tok[b][:, s:s + 1], 0)
                                            ).then_inc(xg_in[b], 16)

            def put(m, b):
                j = 2 * m + b
                waits_apart(pool, (dest_ready, j + 1), (y_ready, j + 1))
                for s in range(SUB):
                    waits_apart(pool, (y_put, 16 * (SUB * j + s)))
                    pool.indirect_dma_start(y_rows, bass.IndirectOffsetOnAxis(dest[b][:, s:s + 1], 0),
                                            y_out[b][:, s, :], None, bounds_check=K * N - 1,
                                            oob_is_err=False).then_inc(y_put, 16)

            gather(0, 0)
            gather(0, 1)
            gather(1, 0)
            gather(1, 1)
            with pool.Fori(2, LAST) as m:
                put(m - 2, 0)
                gather(m, 0)
                put(m - 2, 1)
                gather(m, 1)
            put(LAST - 2, 0)
            gather(LAST, 0)
            put(LAST - 2, 1)
            put(LAST - 1, 0)
            put(LAST - 1, 1)
            put(LAST, 0)

        @block.scalar
        def _(act):
            def cur_high(g):
                act.wait_ge(ln_ready, g + 1)
                sl = slice(g * LNT, (g + 1) * LNT)
                act.activation(ch[:, sl, 0:D], xall[:, sl, :], ACT.Copy).then_inc(ch_ready, 1)

            def make_high(i, k):
                n = 4 * i + k
                wait(act, adj_in[k], 16 * (i + 1))
                wait(act, unit_done, n - 1)
                act.activation(high[k % 2], adj_sb[:, k, :], ACT.Copy).then_inc(high_ready, 1)

            def scale_mask(t, u):
                wait(act, hscale_ready, t + 1)
                wait(act, num_ready, t - 1)
                act.activation(wm[:, u, 0:D + 1], acc_mask[u][:, 0:D + 1], ACT.Copy,
                               scale=hscale[:, u:u + 1]).then_inc(wm_ready, 1)

            def copy_turned(t, u):
                wait(act, turn_ready, t + 1)
                wait(act, logits_ready, t - 1)
                act.activation(xnT[:, u, :], turned[u], ACT.Copy).then_inc(xnT_ready, 1)

            def exps(i):
                wait(act, z_ready, i + 1)
                act.activation(ez[:, :, :], z[:, :, :], ACT.Exp).then_inc(exp_ready, 1)

            def body(i):
                later = not (isinstance(i, int) and i == 0)
                if not later:
                    cur_high(0)
                make_high(i, 0)
                if later:
                    scale_mask(2 * i - 1, 1)
                else:
                    cur_high(1)
                make_high(i, 1)
                if not later:
                    cur_high(2)
                    cur_high(3)
                if later:
                    copy_turned(2 * i - 1, 1)
                make_high(i, 2)
                if later:
                    exps(i - 1)
                scale_mask(2 * i, 0)
                make_high(i, 3)
                copy_turned(2 * i, 0)

            def tail(i):
                scale_mask(2 * i - 1, 1)
                copy_turned(2 * i - 1, 1)
                exps(i - 1)

            pairs(act, body, tail)

            def hidden(m, b):
                j = 2 * m + b
                e = act.value_load(tile_expert[0:1, bass.ds(j, 1)], min_val=0, max_val=E - 1)
                for q in range(4):
                    wait(act, h1_ready, 4 * j + q + 1)
                    wait(act, hl_ready, 4 * j + q - 3)
                    for f in range(2 * q, 2 * q + 2):
                        ins = act.activation(h32[:, f * TT:(f + 1) * TT],
                                             h1[q][:, (f % 2) * TT:(f % 2 + 1) * TT], ACT.Relu,
                                             bias=b1[:, bass.ds(e * FC + f, 1)])
                    ins.then_inc(relu_ready, 1)

            def x_high(m, b):
                j = 2 * m + b
                wait(act, xt_ready, j + 1)
                wait(act, h1_ready, 4 * (j - 1))
                act.activation(xh[b], xT[b], ACT.Copy).then_inc(xh_ready, 1)

            act.wait_ge(table_ready, 2)
            act.wait_ge(small_in, 48)
            x_high(0, 0)
            hidden(0, 0)
            x_high(0, 1)
            with act.Fori(0, LAST - 1) as m:
                hidden(m, 1)
                x_high(m + 1, 0)
                hidden(m + 1, 0)
                x_high(m + 1, 1)
            hidden(LAST - 1, 1)
            x_high(LAST, 0)
            hidden(LAST, 0)

        @block.vector
        def _(dve):
            steps = [0]

            def then(ins, i=None, per=0, apart=False):
                steps[0] += 1
                ins.then_inc(dve_step, 1)
                value = steps[0] if i is None else steps[0] + i * per
                if apart:
                    waits_apart(dve, (dve_step, value))
                else:
                    dve.wait_ge(dve_step, value)

            dve.memset(zero[:, :], 0.0).then_inc(dconst, 1)
            dve.wait_ge(consts, 11)
            dve.tensor_scalar(pad_codes[:, :], pad_codes[:, :], TT - 1, K * N, ALU.bitwise_and,
                              ALU.bitwise_or).then_inc(dconst, 1)
            then(dve.tensor_copy(count[:, :], base[:, :]))

            def rsqrt(y, v, a, i=None, per=0):
                then(dve.tensor_scalar(y.bitcast(I32), v.bitcast(I32), 1, None, ALU.arith_shift_right), i, per)
                then(dve.tensor_scalar(y.bitcast(I32), y.bitcast(I32), -1, RSQRT_BITS, ALU.mult, ALU.add), i, per)
                for n in range(3):
                    then(dve.scalar_tensor_tensor(a, y, -0.5, y, ALU.mult, ALU.mult), i, per)
                    then(dve.tensor_tensor(a, a, v, ALU.mult), i, per)
                    ins = dve.scalar_tensor_tensor(y, a, 1.5, y, ALU.add, ALU.mult)
                    if n < 2:
                        then(ins, i, per)
                return ins

            def norm_group(g):
                dve.wait_ge(x_all_in[g], 16)
                for t in range(g * LNT, (g + 1) * LNT):
                    dve.bn_stats(stats[:, t, :], xall[:, t, :]).then_inc(dve_step, 1)
                steps[0] += LNT
                dve.wait_ge(dve_step, steps[0])
                for t in range(g * LNT, (g + 1) * LNT):
                    dve.bn_aggr(mv[:, t, :], stats[:, t, :]).then_inc(dve_step, 1)
                steps[0] += LNT
                dve.wait_ge(dve_step, steps[0])
                sl = slice(g * LNT, (g + 1) * LNT)
                then(dve.tensor_scalar(var[:, sl], mv[:, sl, 1], EPS, None, ALU.add))
                then(rsqrt(rstd[:, sl], var[:, sl], newton[:, sl]))
                for t in range(g * LNT, (g + 1) * LNT):
                    ins = dve.tensor_scalar(xall[:, t, :], xall[:, t, :], mv[:, t, 0:1], rstd[:, t:t + 1],
                                            ALU.subtract, ALU.mult)
                ins.then_inc(ln_ready, 1)

            def make_mask(i, k):
                n = 4 * i + k
                wait(dve, adj_in[k], 16 * (i + 1))
                wait(dve, unit_done, n - 1)
                dve.tensor_scalar(mask[k % 2], adj_sb[:, k, :], 0.0, None, ALU.is_gt).then_inc(mask_ready, 1)

            def make_low(i, k):
                wait(dve, high_ready, 4 * i + k + 1)
                dve.tensor_tensor(low[k % 2], adj_sb[:, k, :], high[k % 2],
                                  ALU.subtract).then_inc(low_ready, 1)

            def residual(i, t, u, per):
                lag = u
                wait(dve, unit_done, 2 * t + 2)
                one, w = slice(u, u + 1), slice(2 + u, 3 + u)
                then(dve.tensor_scalar(var[:, one], acc_mask[u][:, D:D + 1], 1e-24, None, ALU.max), i, per)
                rsqrt(hscale[:, one], var[:, one], newton[:, one], i, per).then_inc(hscale_ready, 1)
                wait(dve, wm_ready, t + 1)
                dve.tensor_tensor(num[:, u, 0:D + 1], wm[:, u, 0:D + 1], acc_adj[u][:, 0:D + 1],
                                  ALU.add).then_inc(num_ready, 1)
                wait(dve, num_ready, t + 1)
                then(dve.reciprocal(rec[:, u:u + 1], num[:, u, D:D + 1]), i, per)
                wait(dve, x_in[u], 16 * (i + 1 - lag))
                wait(dve, rows_out[u], 32 * (i - lag))
                wait(dve, turn_ready, t - 1)
                then(dve.scalar_tensor_tensor(x1t[:, u, :], num[:, u, 0:D], rec[:, u:u + 1], xt[:, u, :],
                                              ALU.mult, ALU.add), i, per)
                then(dve.bn_stats(st2[:, u, :], x1t[:, u, :]), i, per, apart=True)
                then(dve.bn_aggr(mv2[:, u, :], st2[:, u, :]), i, per)
                then(dve.tensor_scalar(var[:, w], mv2[:, u, 1:2], EPS, None, ALU.add), i, per)
                then(rsqrt(rs2[:, one], var[:, w], newton[:, w], i, per), i, per)
                dve.tensor_scalar(xnt[:, u, :], x1t[:, u, :], mv2[:, u, 0:1], rs2[:, u:u + 1],
                                  ALU.subtract, ALU.mult).then_inc(xn_ready, 1)

            def by_e(a):
                return a.unsqueeze(2).to_broadcast([P, 2, E])

            kv_b = kv[:, :].unsqueeze(1).to_broadcast([P, 2, E])

            def choose(c, pr, best, i, per):
                then(dve.tensor_reduce(best[:, :], pr[:, :, :], AX, ALU.max), i, per)
                then(dve.tensor_tensor(eq[:, :, :], pr[:, :, :], by_e(best[:, :]), ALU.is_equal), i, per)
                then(dve.tensor_tensor(eq[:, :, :], eq[:, :, :], kv_b, ALU.mult), i, per)
                then(dve.tensor_reduce(km[:, :], eq[:, :, :], AX, ALU.max), i, per)
                then(dve.tensor_tensor(oh[:, c, :, :], kv_b, by_e(km[:, :]), ALU.is_equal), i, per)

            def route(i, pair, per):
                wait(dve, logits_ready, 2 * pair + 2)
                then(dve.tensor_reduce(mx[:, :], logits, AX, ALU.max), i, per)
                dve.tensor_tensor(z[:, :, :], logits, by_e(mx[:, :]), ALU.subtract).then_inc(z_ready, 1)
                wait(dve, exp_ready, pair + 1)
                then(dve.tensor_reduce(sm[:, :], ez[:, :, :], AX, ALU.add), i, per)
                then(dve.reciprocal(sm[:, :], sm[:, :]), i, per)
                then(dve.tensor_tensor(prob[:, :, :], ez[:, :, :], by_e(sm[:, :]), ALU.mult), i, per)
                choose(0, prob, m1, i, per)
                then(dve.scalar_tensor_tensor(prob2[:, :, :], oh[:, 0, :, :], -2.0, prob[:, :, :],
                                              ALU.mult, ALU.add), i, per)
                choose(1, prob2, m2, i, per)
                wait(dve, rank_ready, pair)
                dve.tensor_tensor(sel[:, :, :], oh[:, 0, :, :], oh[:, 1, :, :], ALU.add).then_inc(sel_ready, 1)
                then(dve.scalar_tensor_tensor(sm[:, :], m1[:, :], 1e-9, m2[:, :], ALU.add, ALU.add), i, per)
                then(dve.reciprocal(sm[:, :], sm[:, :]), i, per)
                for c, m in enumerate((m1, m2)):
                    then(dve.tensor_tensor(gates[:, bass.ds(2 * pair, 2), c], m[:, :], sm[:, :], ALU.mult),
                         i, per)

            def list_places(i, pair, per):
                wait(dve, rank_ready, pair + 1)
                then(dve.tensor_tensor(pos[:, :, :], rank, count[:, :].unsqueeze(1).to_broadcast([P, 2, E]),
                                       ALU.add), i, per)
                then(dve.tensor_tensor(count[:, :], count[:, :], total, ALU.add), i, per)
                then(dve.tensor_tensor(place[:, :, :, :], oh[:, :, :, :],
                                       pos[:, :, :].unsqueeze(1).to_broadcast([P, 2, 2, E]), ALU.mult), i, per)
                wait(dve, code_put, 64 * pair)
                then(dve.tensor_scalar(codes[:, :, :], codes[:, :, :], 4 * P, None, ALU.add), i, per)
                with nc.allow_low_precision(reason="row numbers are whole and below 2^24"):
                    dve.tensor_reduce(slots[:, :, :], place[:, :, :, :], AX, ALU.add).then_inc(slots_ready, 1)

            def body(i, per, lag=True):
                make_mask(i, 0)
                make_low(i, 0)
                if lag:
                    residual(i, 2 * i - 1, 1, per)
                make_mask(i, 1)
                make_low(i, 1)
                make_mask(i, 2)
                make_low(i, 2)
                if lag:
                    route(i, i - 1, per)
                residual(i, 2 * i, 0, per)
                make_mask(i, 3)
                make_low(i, 3)
                if lag:
                    list_places(i, i - 1, per)

            norm_group(0)
            make_mask(0, 0)
            make_low(0, 0)
            norm_group(1)
            make_mask(0, 1)
            make_low(0, 1)
            norm_group(2)
            norm_group(3)
            for k in (2,):
                make_mask(0, k)
                make_low(0, k)
            residual(0, 0, 0, 0)
            make_mask(0, 3)
            make_low(0, 3)
            per = 27 * 2 + 1 + 3 + 5 + 1 + 5 + 4 + 4
            at_loop = steps[0]
            with dve.Fori(1, NPAIR) as i:
                steps[0] = at_loop - per
                body(i, per)
                assert steps[0] == at_loop, (steps[0], at_loop)
            steps[0] = at_loop + per * (NPAIR - 1)
            residual(NPAIR, NT - 1, 1, 0)
            route(NPAIR, NPAIR - 1, 0)
            list_places(NPAIR, NPAIR - 1, 0)

            then(dve.tensor_tensor(nt_f[:, :], count[:, :], base[:, :], ALU.subtract))
            then(dve.tensor_scalar(nt_i[:, :], nt_f[:, :], 1.0, TT - 1.0, ALU.max, ALU.add))
            then(dve.tensor_scalar(nt_i[:, :], nt_i[:, :], TT.bit_length() - 1, None, ALU.arith_shift_right))
            then(dve.tensor_copy(nt_f[:, :], nt_i[:, :]))
            then(dve.tensor_copy(end[:, :], nt_f[:, :]))
            for e in range(1, E):
                then(dve.tensor_tensor(end[:, e:e + 1], end[:, e - 1:e], end[:, e:e + 1], ALU.add))
            then(dve.tensor_scalar(jump[:, :], nt_f[:, :], -float(TT), float(EROWS), ALU.mult, ALU.add))

            def row_b(a):
                return a[0:1, :].unsqueeze(1).to_broadcast([1, TILES, E])

            then(dve.tensor_tensor(past[:, :, :], ti[:, :].unsqueeze(2).to_broadcast([1, TILES, E]),
                                   row_b(end), ALU.is_ge))
            then(dve.tensor_tensor(pj[:, :, :], past[:, :, :], row_b(jump), ALU.mult))
            then(dve.tensor_reduce(te[:, :], past[:, :, :], AX, ALU.add))
            then(dve.tensor_reduce(tr[:, :], pj[:, :, :], AX, ALU.add))
            dve.tensor_scalar(tile_expert[:, :], te[:, :], float(E - 1), None, ALU.min).then_inc(table_ready, 1)
            dve.scalar_tensor_tensor(tile_row[:, :], ti[:, :], float(TT), tr[:, :], ALU.mult,
                                     ALU.add).then_inc(table_ready, 1)

            def tokens(m, b):
                j = 2 * m + b
                wait(dve, codes_in[b], 16 * (m + 1))
                wait(dve, xg_in[b], 16 * SUB * m)
                dve.tensor_scalar(tok[b][:, :], tcodes[:, bass.ds(j, 1), :].rearrange("p a s -> p (a s)"),
                                  1, None, ALU.arith_shift_right).then_inc(tok_ready, 1)

            def x_low(m, b):
                j = 2 * m + b
                wait(dve, xh_ready, j + 1)
                dve.tensor_tensor(xl[b], xT[b], xh[b], ALU.subtract).then_inc(xl_ready, 1)

            def h_parts(m, b):
                j = 2 * m + b
                wait(dve, yp_ready, j - 1)
                for q in range(4):
                    s = slice(q * 512, (q + 1) * 512)
                    wait(dve, relu_ready, 4 * j + q + 1)
                    dve.tensor_copy(hh[b][:, s], h32[:, s]).then_inc(hh_ready, 1)
                    wait(dve, hh_ready, 4 * j + q + 1)
                    dve.tensor_tensor(hl[b][:, s], h32[:, s], hh[b][:, s], ALU.subtract).then_inc(hl_ready, 1)

            def outputs(m, b):
                j = 2 * m + b
                e = dve.value_load(tile_expert[0:1, bass.ds(j, 1)], min_val=0, max_val=E - 1)
                wait(dve, yp_ready, j + 1)
                wait(dve, y_put, 16 * SUB * (j - 1))
                dve.tensor_copy(dest[b][:, :], tcodes[:, bass.ds(j, 1), :].rearrange("p a s -> p (a s)")
                                ).then_inc(dest_ready, 1)
                dve.tensor_tensor(y_out[b], yp[b].rearrange("p (s d) -> p s d", s=SUB),
                                  b2[:, bass.ds(e, 1), :].to_broadcast([P, SUB, D]),
                                  ALU.add).then_inc(y_ready, 1)

            def step(m, b, more_tokens=True, more_x=True):
                if more_tokens:
                    tokens(m + 1, b)
                h_parts(m, b)
                if more_x:
                    x_low(*((m, 1) if b == 0 else (m + 1, 0)))
                if not (isinstance(m, int) and 2 * m + b == 0):
                    outputs(*((m - 1, 1) if b == 0 else (m, 0)))

            tokens(0, 0)
            tokens(0, 1)
            x_low(0, 0)
            step(0, 0)
            step(0, 1)
            with dve.Fori(1, LAST - 1) as m:
                step(m, 0)
                step(m, 1)
            step(LAST - 1, 0)
            step(LAST - 1, 1, more_tokens=False)
            step(LAST, 0, more_tokens=False, more_x=False)
            outputs(LAST, 0)

            def combine(m, b):
                c = 2 * m + b
                wait(dve, yr_in[b], 32 * (m + 1))
                for k, (src, ready) in enumerate(((x1_sb, fin_part), (o_sb, fin_ready))):
                    for t in range(C4):
                        tile = bass.ds(c * C4 + t, 1)

                        def row(a, lo=0):
                            return a[:, tile, lo:lo + D].rearrange("p a d -> p (a d)")

                        if k == 1:
                            wait(dve, fin_part, C4 * c + t + 1)
                        dve.scalar_tensor_tensor(row(o_sb), row(y_sb, k * D), gates[:, tile, k],
                                                 row(src), ALU.mult, ALU.add).then_inc(ready, 1)

            with dve.Fori(0, NC4 // 2) as m:
                combine(m, 0)
                combine(m, 1)

        @block.tensor
        def _(pe):
            pe.wait_ge(consts, 11)
            pe.wait_ge(small_in, 48)

            def unit(i, k):
                n, t, u, h = 4 * i + k, 2 * i + k // 2, k // 2, k % 2
                wait(pe, high_ready, n + 1)
                wait(pe, mask_ready, n + 1)
                wait(pe, low_ready, n + 1)
                if h == 0:
                    wait(pe, num_ready, t - 1)
                for jj in range(UJ):
                    jt = h * UJ + jj
                    if isinstance(i, int) and i == 0 and k < 2 and jt % LNT == 0:
                        pe.wait_ge(cl_ready, jt // LNT + 1)
                    s = slice(jj * P, (jj + 1) * P)
                    a, m = acc_adj[u], acc_mask[u]
                    on, off = jt == 0, jt == NT - 1
                    pe.matmul(a[:, 0:D + 1], high[h][:, s], ch[:, jt, 0:D + 1], start=on, stop=False)
                    pe.matmul(a[:, 0:D], high[h][:, s], cl[:, jt, :], start=False, stop=False)
                    pe.matmul(a[:, 0:D + 1], low[h][:, s], ch[:, jt, 0:D + 1], start=False, stop=off)
                    pe.matmul(m[:, 0:D + 1], mask[h][:, s], ch[:, jt, 0:D + 1], start=on, stop=False)
                    ins = pe.matmul(m[:, 0:D], mask[h][:, s], cl[:, jt, :], start=False, stop=off)
                ins.then_inc(unit_done, 1)

            def turn(t, u):
                wait(pe, xn_ready, t + 1)
                wait(pe, xnT_ready, t - 1)
                for c in range(DC):
                    ins = pe.transpose(turned[u][:, c * P:(c + 1) * P], xnt[:, u, c * P:(c + 1) * P],
                                       ident[:, :])
                ins.then_inc(turn_ready, 1)

            def router(t, u, pair):
                wait(pe, xnT_ready, t + 1)
                wait(pe, z_ready, pair)
                for c in range(DC):
                    ins = pe.matmul(logits[:, u, :], xnT[:, u, c * P:(c + 1) * P], rw[:, c, :],
                                    start=(c == 0), stop=(c == DC - 1))
                ins.then_inc(logits_ready, 1)

            def ranks(pair):
                wait(pe, sel_ready, pair + 1)
                wait(pe, slots_ready, pair)
                pe.matmul(rank[:, 0, :], tri[:, :], sel[:, 0, :], start=True, stop=True)
                pe.matmul(rank[:, 1, :], tri[:, :], sel[:, 1, :], start=True, stop=False)
                pe.matmul(rank[:, 1, :], ones[:, :], sel[:, 0, :], start=False, stop=True)
                pe.matmul(total, ones[:, :], sel[:, 0, :], start=True, stop=False)
                pe.matmul(total, ones[:, :], sel[:, 1, :], start=False, stop=True).then_inc(rank_ready, 1)

            def body(i):
                lag = not (isinstance(i, int) and i == 0)
                unit(i, 0)
                if lag:
                    turn(2 * i - 1, 1)
                unit(i, 1)
                if lag:
                    router(2 * i - 1, 1, i - 1)
                unit(i, 2)
                if lag:
                    ranks(i - 1)
                turn(2 * i, 0)
                unit(i, 3)
                router(2 * i, 0, i)

            def tail(i):
                turn(2 * i - 1, 1)
                router(2 * i - 1, 1, i - 1)
                ranks(i - 1)

            pairs(pe, body, tail)

            def part(e, which, f0, n):
                return W[:, bass.ds(e, 1), which * MATS + f0:which * MATS + f0 + n].rearrange("p a n -> p (a n)")

            def hidden(m, b):
                j = 2 * m + b
                e = pe.value_load(tile_expert[0:1, bass.ds(j, 1)], min_val=0, max_val=E - 1)
                wait(pe, xl_ready, j + 1)
                for q in range(4):
                    wait(pe, relu_ready, 4 * j + q - 3)
                    for f in range(2 * q, 2 * q + 2):
                        o = h1[q][:, (f % 2) * TT:(f % 2 + 1) * TT]
                        for c in range(DC):
                            cs = slice(c * TT, (c + 1) * TT)
                            w1h, w1l = (part(e, w, c * DFF + f * P, P) for w in (0, 1))
                            pe.matmul(o, w1h, xh[b][:, cs], start=(c == 0), stop=False)
                            pe.matmul(o, w1h, xl[b][:, cs], start=False, stop=False)
                            ins = pe.matmul(o, w1l, xh[b][:, cs], start=False, stop=(c == DC - 1))
                    ins.then_inc(h1_ready, 1)

            def x_turn(m, b):
                j = 2 * m + b
                wait(pe, xg_in[b], 16 * SUB * (m + 1))
                wait(pe, xl_ready, j - 1)
                for s in range(SUB):
                    for c in range(DC):
                        ins = pe.transpose(xT[b][:, c * TT + s * P:c * TT + (s + 1) * P],
                                           xg[b][:, s, c * P:(c + 1) * P], ident[:, :])
                ins.then_inc(xt_ready, 1)

            def second(m, b):
                j = 2 * m + b
                e = pe.value_load(tile_expert[0:1, bass.ds(j, 1)], min_val=0, max_val=E - 1)
                wait(pe, y_ready, j - 1)
                for s in range(SUB):
                    for f in range(FC):
                        if s == 0 and f % 2 == 0:
                            wait(pe, hl_ready, 4 * j + f // 2 + 1)
                        fs = slice(f * TT + s * P, f * TT + (s + 1) * P)
                        o = yp[b][:, s * D:(s + 1) * D]
                        w2h, w2l = (part(e, w, f * D, D) for w in (2, 3))
                        pe.matmul(o, hh[b][:, fs], w2h, start=(f == 0), stop=False)
                        pe.matmul(o, hl[b][:, fs], w2h, start=False, stop=False)
                        ins = pe.matmul(o, hh[b][:, fs], w2l, start=False, stop=(f == FC - 1))
                ins.then_inc(yp_ready, 1)

            def step(m, b, more=True):
                hidden(m, b)
                if more:
                    x_turn(*((m, 1) if b == 0 else (m + 1, 0)))
                if not (isinstance(m, int) and 2 * m + b == 0):
                    second(*((m - 1, 1) if b == 0 else (m, 0)))

            pe.wait_ge(table_ready, 2)
            x_turn(0, 0)
            pe.wait_ge(w_in[0], 16)
            step(0, 0)
            pe.wait_ge(w_in[1], 16)
            step(0, 1)
            for e in range(2, E):
                pe.wait_ge(w_in[e], 16)
            with pe.Fori(1, LAST) as m:
                step(m, 0)
                step(m, 1)
            step(LAST, 0, more=False)
            second(LAST, 0)


def kernel(x, adj, L0_ffn_router_w, L0_ffn_w1_all, L0_ffn_b1_all, L0_ffn_w2_all, L0_ffn_b2_all):
    import numpy as np
    import concourse.bacc as bacc
    from concourse.bass_utils import run_bass_kernel_spmd as run

    a = np.asarray
    c = np.ascontiguousarray
    adj_u = c(a(adj).reshape(NPAIR, 2, P, 2, UJ, P).transpose(0, 1, 3, 5, 4, 2)).reshape(NPAIR, 4, P, UNIT)
    w1 = a(L0_ffn_w1_all).reshape(E, DFF, DC, P).transpose(3, 0, 2, 1).reshape(P, E, 1, MATS)
    w2 = a(L0_ffn_w2_all).reshape(E, D, FC, P).transpose(3, 0, 2, 1).reshape(P, E, 1, MATS)
    arrays = {
        "x": c(a(x)),
        "adj_u": adj_u,
        "w_all": c(np.concatenate([w1, w2], axis=2)).reshape(P, E * 2 * MATS),
        "b1_t": c(a(L0_ffn_b1_all).reshape(E, FC, P).transpose(2, 0, 1)).reshape(P, E * FC),
        "b2_r": c(a(L0_ffn_b2_all)).reshape(1, E, D),
        "rw_t": c(a(L0_ffn_router_w).reshape(E, DC, P).transpose(2, 1, 0)),
    }
    nc = bacc.Bacc("TRN2", target_bir_lowering=False, num_devices=1)
    args = {k: nc.dram_tensor(k, v.shape, mybir.dt.from_np(v.dtype), kind="ExternalInput").ap()
            for k, v in arrays.items()}
    out = nc.dram_tensor("out", (N, D), F32, kind="ExternalOutput").ap()
    moe_gnn_kernel(nc, out=out, **args)
    r = run(nc, [arrays], core_ids=[0])
    return r.results[0]["out"]
```

```python
from contextlib import ExitStack

import concourse.bass as bass
from concourse import mybir

P = 128
F32 = mybir.dt.float32
F16 = mybir.dt.float16
BF16 = mybir.dt.bfloat16
I32 = mybir.dt.int32
ALU = mybir.AluOpType
ACT = mybir.ActivationFunctionType
AX = mybir.AxisListType.X

N, D, DFF, E, K = 4096, 256, 1024, 8, 2
NT = N // P
NPAIR = NT // 2
UJ = NT // 2
UNIT = UJ * P
DC = D // P
FC = DFF // P
EPS = 1e-5
RSQRT_BITS = 0x5F3759DF
LNG = 4
LNT = NT // LNG

TT = 256
SUB = TT // P
TILES = (K * N + (TT - 1) * E) // TT
EROWS = N
ROWS = E * EROWS + (TILES - E) * TT
PADQ = ROWS // P
HE = E // 2
HM = 2 * HE
MATS = DC * DFF
EW = 4 * MATS
CH = MATS // 2
LAST = (TILES - 1) // 2

SX = 264


def moe_gnn_kernel(nc, x, adj_u, w_all, b1_t, b2_r, rw_t, out):
    with ExitStack() as ctx:
        def sb(name, shape, dt=F32):
            return ctx.enter_context(nc.sbuf_tensor(name, shape, dt))

        def sem(name):
            return ctx.enter_context(nc.semaphore(name))

        def dram(name, shape, dt=F32):
            return nc.dram_tensor(name, shape, dt).ap()

        w_split = dram("w_split", (P, E - HE, EW), F16)
        xn_rows = dram("xn_rows", (N + TT, 2 * D), F16)
        table = dram("table", (ROWS, 2), I32)

        W = sb("W", [P, E, EW], F16)
        Wf = W[:, :, :].rearrange("p e n -> p (e n)")
        lower = Wf[:, 0:4 * EW]
        upper = Wf[:, 4 * EW:8 * EW]
        xall = lower[:, 0:2 * NT * D].bitcast(F32).rearrange("p (t d) -> p t d", t=NT)
        adj_sb = upper[:, 0:4 * 2 * UNIT].bitcast(F32).rearrange("p (k n) -> p k n", k=4)
        at = 4 * 2 * UNIT
        parts = []
        for _ in range(6):
            parts.append(upper[:, at:at + UNIT])
            at += UNIT
        high, low, mask = parts[0:2], parts[2:4], parts[4:6]
        mask = [m.bitcast(BF16) for m in mask]
        pads = upper[:, at:at + 4 * PADQ].bitcast(I32).rearrange("p (q w) -> p q w", w=2)
        W_mats = W[:, :, :].rearrange("p e (m h n) -> p (e m) h n", m=2, h=2)

        R = sb("R", [P, NT * SX + NT * D], F16)
        ch = R[:, 0:NT * SX].rearrange("p (t d) -> p t d", t=NT)
        cl = R[:, NT * SX:].rearrange("p (t d) -> p t d", t=NT)
        Rf = R[:, :]
        at = 0

        def region(n, dt):
            nonlocal at
            words = n if dt == F16 else 2 * n
            v = Rf[:, at:at + words]
            at += words
            return v if dt == F16 else v.bitcast(dt)

        hh = [region(FC * TT, F16) for _ in range(2)]
        hl = [region(FC * TT, F16) for _ in range(2)]
        h32 = region(FC * TT, F32)
        xg = [region(SUB * 2 * D, F16).rearrange("p (s d) -> p s d", s=SUB) for _ in range(2)]
        xs = [region(2 * DC * TT, F16) for _ in range(2)]
        assert at <= NT * (SX + D)

        stage = sb("stage", [P, 2, CH])
        stage_h = sb("stage_h", [P, 2, CH], F16)
        stage_l = sb("stage_l", [P, 2, CH], F16)
        y_out = [stage[:, b, 0:SUB * D].rearrange("p (s d) -> p s d", s=SUB) for b in range(2)]
        y32 = [stage[:, b, SUB * D:2 * SUB * D].rearrange("p (s d) -> p s d", s=SUB) for b in range(2)]
        b2 = sb("b2", [P, E, D])
        b1 = sb("b1", [P, E * FC])
        rw = sb("rw", [P, DC, E])
        xt = sb("xt", [P, 2, D])
        x1t = sb("x1t", [P, 2, D])
        xnt = sb("xnt", [P, 2, D])
        xnt_hl = sb("xnt_hl", [P, 2, 2 * D], F16)
        xnT = sb("xnT", [P, 2 * D])
        sums = sb("sums", [P, 2, 2, SX])
        num = sb("num", [P, 2, SX])
        zero = sb("zero", [P, D])
        ident = sb("ident", [P, P])
        ident16 = sb("ident16", [P, P], F16)
        tri = sb("tri", [P, P], BF16)
        ones = sb("ones", [P, P], BF16)
        stats = sb("stats", [P, NT, 6])
        mv = sb("mv", [P, NT, 2])
        rstd = sb("rstd", [P, NT])
        var = sb("var", [P, NT])
        newton = sb("newton", [P, NT])
        hscale = sb("hscale", [P, 2])
        rec = sb("rec", [P, 2])
        st2 = sb("st2", [P, 2, 6])
        mv2 = sb("mv2", [P, 2, 2])
        rs2 = sb("rs2", [P, 2])
        kv = sb("kv", [P, E])
        z = sb("z", [P, 2, E])
        ez = sb("ez", [P, 2, E])
        prob = sb("prob", [P, 2, E])
        prob2 = sb("prob2", [P, 2, E])
        eq = sb("eq", [P, 2, E])
        oh = sb("oh", [P, 2, 2, E])
        sel = sb("sel", [P, 2, E], BF16)
        mx = sb("mx", [P, 2])
        m1 = sb("m1", [P, 2])
        m2 = sb("m2", [P, 2])
        km = sb("km", [P, 2])
        sm = sb("sm", [P, 2])
        gates = sb("gates", [P, K, 2])
        count = sb("count", [P, E])
        pos = sb("pos", [P, 2, E])
        place = sb("place", [P, 2, 2, E])
        slots = sb("slots", [P, 2, 2], I32)
        entry = sb("entry", [P, 2, 2, 2], I32)
        base = sb("base", [P, E])
        nt_i = sb("nt_i", [P, E], I32)
        nt_f = sb("nt_f", [P, E])
        end = sb("end", [P, E])
        jump = sb("jump", [P, E])
        ti = sb("ti", [1, TILES])
        past, pj = (a[0:1, 0:TILES * E].rearrange("p (t e) -> p t e", e=E) for a in (
            num[:, :, :].rearrange("p u d -> p (u d)"), sums[:, :, :, :].rearrange("p u s d -> p (u s d)")))
        te = sb("te", [1, TILES])
        tr = sb("tr", [1, TILES])
        tile_expert = sb("tile_expert", [1, TILES], I32)
        tile_row = sb("tile_row", [1, TILES], I32)
        listed = sb("listed", [P, TILES, SUB, 2], I32)
        mark = sb("mark", [P, 1])
        tok = [sb(f"tok{b}", [P, SUB], I32) for b in range(2)]
        dest = [sb(f"dest{b}", [P, SUB], I32) for b in range(2)]
        gate = [sb(f"gate{b}", [P, SUB]) for b in range(2)]

        PS = ctx.enter_context(nc.psum_tensor("PS", [P, 8, 512], F32))
        acc = [PS[:, 2 * u:2 * u + 2, :] for u in range(2)]
        turned = PS[:, 4, :]
        logits = PS[:, 6, 0:2 * E].rearrange("p (u e) -> p u e", u=2)
        rank = PS[:, 7, 0:2 * E].rearrange("p (u e) -> p u e", u=2)
        total = PS[:, 7, 2 * E:3 * E]
        h1 = [PS[:, q, :] for q in range(4)]
        yp = [PS[:, 4, :], PS[:, 5, :]]
        xT = [PS[:, 6, :].bitcast(F16), PS[:, 7, :].bitcast(F16)]

        adj_in = [sem(f"adj_in{k}") for k in range(4)]
        x_all_in = [sem(f"x_all_in{g}") for g in range(LNG)]
        x_in = sem("x_in")
        small_in = sem("small_in")
        wf_in = [sem(f"wf_in{v}") for v in range(2)]
        wsplit_out = [sem(f"wsplit_out{v}") for v in range(2)]
        rows_out = sem("rows_out")
        pads_out = sem("pads_out")
        w_in = sem("w_in")
        table_put = sem("table_put")
        listed_in = [sem(f"listed_in{b}") for b in range(2)]
        xg_in = [sem(f"xg_in{b}") for b in range(2)]
        y_put = sem("y_put")
        consts = sem("consts")
        dconst = sem("dconst")
        ln_ready = sem("ln_ready")
        ch_ready = sem("ch_ready")
        cl_ready = sem("cl_ready")
        high_ready = sem("high_ready")
        mask_ready = sem("mask_ready")
        low_ready = sem("low_ready")
        unit_done = sem("unit_done")
        sums_ready = sem("sums_ready")
        num_ready = sem("num_ready")
        xn_ready = sem("xn_ready")
        nh_ready = sem("nh_ready")
        nl_ready = sem("nl_ready")
        turn_ready = sem("turn_ready")
        xnT_ready = sem("xnT_ready")
        logits_ready = sem("logits_ready")
        z_ready = sem("z_ready")
        exp_ready = sem("exp_ready")
        sel_ready = sem("sel_ready")
        rank_ready = sem("rank_ready")
        slots_ready = sem("slots_ready")
        whigh_ready = sem("whigh_ready")
        wlow_ready = sem("wlow_ready")
        tiles_ready = sem("tiles_ready")
        tok_ready = sem("tok_ready")
        xt_ready = sem("xt_ready")
        xs_ready = sem("xs_ready")
        h1_ready = sem("h1_ready")
        relu_ready = sem("relu_ready")
        hh_ready = sem("hh_ready")
        hl_ready = sem("hl_ready")
        yp_ready = sem("yp_ready")
        y_step = sem("y_step")
        y_ready = sem("y_ready")
        dve_step = sem("dve_step")

        def wait(eng, s, value):
            if isinstance(value, int) and value <= 0:
                return
            eng.wait_ge(s, value)

        def waits_apart(eng, *pairs):
            pairs = [(s, v if isinstance(v, int) else eng.to_reg(v)) for s, v in pairs]
            if not all(isinstance(v, int) for _, v in pairs):
                eng.wait_ge(consts, 12)
            for s, v in pairs:
                wait(eng, s, v)


        def pairs(eng, body, *phases):
            body(0)
            body(1)
            for first, last in phases or [(2, NPAIR)]:
                with eng.Fori(first, last) as i:
                    body(i)

        def at_least(i, n):
            return not isinstance(i, int) or i >= n

        block = ctx.enter_context(nc.Block())

        @block.sync
        def _(sp):
            def load_unit(i, k):
                sp.dma_start(adj_sb[:, k, :],
                             adj_u[bass.ds(i, 1), k].rearrange("a p n -> p (a n)")).then_inc(adj_in[k], 16)

            def load_x(i):
                sp.dma_start(xt[:, :, :], x[bass.ds(i * 2 * P, 2 * P), :].rearrange("(u p) d -> p u d", u=2)
                             ).then_inc(x_in, 16)

            def load_w(c, v):
                sp.dma_start(stage[:, v, :], w_all[:, bass.ds(c * CH, CH)]).then_inc(wf_in[v], 16)

            def store_rows(i):
                rows = bass.ds(i * 2 * P, 2 * P)
                wait(sp, nl_ready, i + 1)
                sp.dma_start(xn_rows[rows, :].rearrange("(u p) d -> p u d", u=2),
                             xnt_hl[:, :, :]).then_inc(rows_out, 16)
                sp.dma_start(out[rows, :].rearrange("(u p) d -> p u d", u=2),
                             x1t[:, :, :]).then_inc(rows_out, 16)

            x_v = x.rearrange("(t p) d -> p t d", p=P)
            for g in range(LNG):
                sp.dma_start(xall[:, g * LNT:(g + 1) * LNT, :],
                             x_v[:, g * LNT:(g + 1) * LNT, :]).then_inc(x_all_in[g], 16)
                load_unit(0, g)
            sp.dma_start(rw[:, :, :], rw_t).then_inc(small_in, 16)
            sp.dma_start(b1[:, :], b1_t).then_inc(small_in, 16)
            sp.dma_start(b2[:, :, :], b2_r.to_broadcast([P, E, D])).then_inc(small_in, 16)
            load_x(0)
            for v in range(2):
                load_w(v, v)
            sp.wait_ge(dconst, 3)
            for s in range(SUB):
                rows = slice(N + s * P, N + (s + 1) * P)
                sp.dma_start(out[rows, :], zero[:, :]).then_inc(pads_out, 16)
                sp.dma_start(xn_rows[rows, :], zero[:, :].bitcast(F16)).then_inc(pads_out, 16)

            def store_split(i, v):
                to = w_split.rearrange("p e (m h n) -> p (e m) h n", m=2, h=2)
                for h, part in enumerate((stage_h, stage_l)):
                    sp.dma_start(to[:, bass.ds(i - HM, 1), h, v * CH:(v + 1) * CH].rearrange("p a n -> p (a n)"),
                                 part[:, v, :]).then_inc(wsplit_out[v], 16)

            def body(i, more=True, upper_half=False):
                for k in range(4):
                    if more:
                        wait(sp, low_ready, 4 * i + k + 1)
                        load_unit(i + 1, k)
                    if k in (1, 3):
                        v = k // 2
                        wait(sp, wlow_ready, 2 * i + v + 1)
                        if upper_half:
                            store_split(i, v)
                        if more:
                            load_w(2 * (i + 1) + v, v)
                if at_least(i, 1):
                    store_rows(i - 1)
                    load_x(i)

            body(0)
            body(1)
            with sp.Fori(2, HM) as i:
                body(i)
            with sp.Fori(HM, NPAIR - 1) as i:
                body(i, upper_half=True)
            body(NPAIR - 1, more=False, upper_half=True)

            def load_expert(e):
                if e > HE:
                    sp.wait_ge(w_in, 16 * e)
                sp.dma_start(W[:, e, :], w_split[:, e - HE, :]).then_inc(w_in, 16)

            def load_list(m, b):
                j = 2 * m + b
                row = sp.value_load(tile_row[0:1, bass.ds(j, 1)], min_val=0, max_val=ROWS - TT)
                wait(sp, listed_in[b], 16 * m)
                sp.dma_start(listed[:, bass.ds(j, 1), :, :].rearrange("p a s w -> p (a s w)"),
                             table[bass.ds(row, TT), :].rearrange("(p s) w -> p (s w)", s=SUB)
                             ).then_inc(listed_in[b], 16)

            for v in range(2):
                sp.wait_ge(wsplit_out[v], 32 * (NPAIR - HM))
            sp.wait_ge(w_in, 16 * HE)
            sp.wait_ge(unit_done, 2 * NT)
            load_expert(HE)
            store_rows(NPAIR - 1)
            sp.wait_ge(tiles_ready, 2)
            sp.wait_ge(table_put, 16 * (4 * NPAIR + 1))
            for m in range(4):
                load_list(m, 0)
                load_list(m, 1)
                if m > 0:
                    load_expert(HE + m)
            with sp.Fori(4, LAST) as m:
                load_list(m, 0)
                load_list(m, 1)
            load_list(LAST, 0)
            sp.wait_ge(y_put, 16 * SUB * TILES)

        @block.gpsimd
        def _(pool):
            pool.memset(ident[:, :], 0.0).then_inc(consts, 1)
            pool.memset(tri[:, :], 1.0).then_inc(consts, 1)
            pool.memset(ones[:, :], 1.0).then_inc(consts, 1)
            pool.memset(ch[:, :, D:D + 2], 1.0).then_inc(consts, 1)
            pool.wait_ge(consts, 2)
            pool.affine_select(out=ident[:, :], in_=ident[:, :], compare_op=ALU.not_equal, fill=1.0,
                               base=0, pattern=[[-1, P]], channel_multiplier=1).then_inc(consts, 1)
            pool.affine_select(out=tri[:, :], in_=tri[:, :], compare_op=ALU.is_gt, fill=0.0,
                               base=0, pattern=[[1, P]], channel_multiplier=-1).then_inc(consts, 1)
            pool.iota(pads[:, :, 0], [[1, PADQ]], base=0, channel_multiplier=PADQ).then_inc(consts, 1)
            pool.iota(entry[:, :, :, 0], [[0, 2], [P, 2]], base=-2 * P, channel_multiplier=1).then_inc(consts, 1)
            pool.iota(kv[:, :], [[-1, E]], base=E, channel_multiplier=0,
                      allow_small_or_imprecise_dtypes=True).then_inc(consts, 1)
            pool.iota(base[:, :], [[EROWS, E]], base=0, channel_multiplier=0,
                      allow_small_or_imprecise_dtypes=True).then_inc(consts, 1)
            pool.iota(ti[:, :], [[1, TILES]], base=0, channel_multiplier=0,
                      allow_small_or_imprecise_dtypes=True).then_inc(consts, 1)

            pool.wait_ge(consts, 11)
            pool.tensor_copy(ident16[:, :], ident[:, :]).then_inc(consts, 1)

            pool.wait_ge(dconst, 3)
            pool.dma_start(table.rearrange("(p q) w -> p q w", p=P), pads[:, :, :]).then_inc(table_put, 16)

            for g in range(LNG):
                pool.wait_ge(ch_ready, g + 1)
                sl = slice(g * LNT, (g + 1) * LNT)
                pool.tensor_tensor(cl[:, sl, :], xall[:, sl, :], ch[:, sl, 0:D],
                                   ALU.subtract).then_inc(cl_ready, 1)

            def split(i, v, upper_half):
                if upper_half:
                    parts = stage_h[:, v, :], stage_l[:, v, :]
                else:
                    parts = (W_mats[:, bass.ds(i, 1), h, v * CH:(v + 1) * CH].rearrange("p a n -> p (a n)")
                             for h in range(2))
                w_high, w_low = parts
                if upper_half and not (isinstance(i, int) and i == HM):
                    waits_apart(pool, (wf_in[v], 16 * (i + 1)), (wsplit_out[v], 32 * (i - HM)))
                else:
                    waits_apart(pool, (wf_in[v], 16 * (i + 1)))
                pool.tensor_copy(w_high, stage[:, v, :]).then_inc(whigh_ready, 1)
                waits_apart(pool, (whigh_ready, 2 * i + v + 1))
                pool.tensor_tensor(w_low, stage[:, v, :], w_high, ALU.subtract).then_inc(wlow_ready, 1)

            def scatter(i):
                waits_apart(pool, (slots_ready, i + 1))
                for c in range(2):
                    for u in range(2):
                        waits_apart(pool, (table_put, 16 * (4 * i + 2 * c + u + 1)))
                        pool.indirect_dma_start(
                            table, bass.IndirectOffsetOnAxis(slots[:, c, u:u + 1], 0),
                            entry[:, c, u, :], None).then_inc(table_put, 16)

            def body(i, upper_half=False):
                split(i, 0, upper_half)
                split(i, 1, upper_half)
                if at_least(i, 2):
                    scatter(i - 2)

            pool.wait_ge(cl_ready, LNG)
            pool.wait_ge(ch_ready, LNG)
            body(0)
            body(1)
            with pool.Fori(2, HM) as i:
                body(i)
            pool.wait_ge(wlow_ready, 2 * HM)
            pool.memset(mark[:, :], 0.0).then_inc(w_in, 16 * HE)
            body(HM, upper_half=True)
            with pool.Fori(HM + 1, NPAIR) as i:
                body(i, upper_half=True)
            scatter(NPAIR - 2)
            scatter(NPAIR - 1)

            def gather(m, b):
                j = 2 * m + b
                waits_apart(pool, (tok_ready, j + 1), (xt_ready, j - 1))
                if isinstance(j, int) and j == 0:
                    pool.wait_ge(rows_out, 32 * NPAIR)
                    pool.wait_ge(pads_out, 16 * 2 * SUB)
                for s in range(SUB):
                    pool.indirect_dma_start(xg[b][:, s, :], None, xn_rows,
                                            bass.IndirectOffsetOnAxis(tok[b][:, s:s + 1], 0)
                                            ).then_inc(xg_in[b], 16)

            def put(m, b):
                j = 2 * m + b
                waits_apart(pool, (y_ready, j + 1))
                for s in range(SUB):
                    waits_apart(pool, (y_put, 16 * (SUB * j + s)))
                    pool.indirect_dma_start(out, bass.IndirectOffsetOnAxis(dest[b][:, s:s + 1], 0),
                                            y_out[b][:, s, :], None, compute_op=ALU.add
                                            ).then_inc(y_put, 16)

            def step(m):
                put(m - 2, 0)
                gather(m, 0)
                put(m - 2, 1)
                gather(m, 1)

            for m in range(2):
                gather(m, 0)
                gather(m, 1)
            step(2)
            with pool.Fori(3, LAST) as m:
                step(m)
            put(LAST - 2, 0)
            gather(LAST, 0)
            put(LAST - 2, 1)
            put(LAST - 1, 0)
            put(LAST - 1, 1)
            put(LAST, 0)

        @block.scalar
        def _(act):
            def cur_high(g):
                act.wait_ge(ln_ready, g + 1)
                sl = slice(g * LNT, (g + 1) * LNT)
                act.activation(ch[:, sl, 0:D], xall[:, sl, :], ACT.Copy).then_inc(ch_ready, 1)

            def make_high(i, k):
                n = 4 * i + k
                wait(act, adj_in[k], 16 * (i + 1))
                wait(act, unit_done, n - 1)
                act.activation(high[k % 2], adj_sb[:, k, :], ACT.Copy).then_inc(high_ready, 1)

            def copy_sums(i, u):
                wait(act, unit_done, 4 * i + 2 * u + 2)
                wait(act, num_ready, i)
                act.activation(sums[:, u, :, 0:D + 1], acc[u][:, :, 0:D + 1], ACT.Copy).then_inc(sums_ready, 1)

            def rows_high(i):
                wait(act, xn_ready, i + 1)
                wait(act, rows_out, 32 * i)
                act.activation(xnt_hl[:, :, 0:D], xnt[:, :, :], ACT.Copy).then_inc(nh_ready, 1)

            def copy_turned(i):
                wait(act, turn_ready, i + 1)
                wait(act, logits_ready, i)
                act.activation(xnT[:, :], turned, ACT.Copy).then_inc(xnT_ready, 1)

            def exps(i):
                wait(act, z_ready, i + 1)
                act.activation(ez[:, :, :], z[:, :, :], ACT.Exp).then_inc(exp_ready, 1)

            def body(i):
                first = not at_least(i, 1)
                if first:
                    cur_high(0)
                make_high(i, 0)
                if at_least(i, 2):
                    exps(i - 2)
                if first:
                    cur_high(1)
                else:
                    copy_sums(i - 1, 1)
                make_high(i, 1)
                if first:
                    cur_high(2)
                    cur_high(3)
                make_high(i, 2)
                if not first:
                    rows_high(i - 1)
                copy_sums(i, 0)
                make_high(i, 3)
                if not first:
                    copy_turned(i - 1)

            pairs(act, body)
            exps(NPAIR - 2)
            copy_sums(NPAIR - 1, 1)
            rows_high(NPAIR - 1)
            copy_turned(NPAIR - 1)
            exps(NPAIR - 1)

            def hidden(m, b):
                j = 2 * m + b
                e = act.value_load(tile_expert[0:1, bass.ds(j, 1)], min_val=0, max_val=E - 1)
                for q in range(4):
                    wait(act, h1_ready, 4 * j + q + 1)
                    wait(act, hl_ready, 4 * j + q - 3)
                    for f in range(2 * q, 2 * q + 2):
                        ins = act.activation(h32[:, f * TT:(f + 1) * TT],
                                             h1[q][:, (f % 2) * TT:(f % 2 + 1) * TT], ACT.Relu,
                                             bias=b1[:, bass.ds(e * FC + f, 1)])
                    ins.then_inc(relu_ready, 1)

            def x_parts(m, b):
                j = 2 * m + b
                wait(act, xt_ready, j + 1)
                wait(act, h1_ready, 4 * (j - 1))
                act.activation(xs[b], xT[b], ACT.Copy).then_inc(xs_ready, 1)

            act.wait_ge(tiles_ready, 2)
            act.wait_ge(small_in, 48)
            x_parts(0, 0)
            hidden(0, 0)
            x_parts(0, 1)
            with act.Fori(0, LAST - 1) as m:
                hidden(m, 1)
                x_parts(m + 1, 0)
                hidden(m + 1, 0)
                x_parts(m + 1, 1)
            hidden(LAST - 1, 1)
            x_parts(LAST, 0)
            hidden(LAST, 0)

        @block.vector
        def _(dve):
            steps = [0]

            def count_step(ins):
                steps[0] += 1
                ins.then_inc(dve_step, 1)

            def then(ins, i=None, per=0, apart=False):
                count_step(ins)
                after(i, per, apart)

            def after(i=None, per=0, apart=False):
                value = steps[0] if i is None else steps[0] + i * per
                if apart:
                    waits_apart(dve, (dve_step, value))
                else:
                    dve.wait_ge(dve_step, value)

            dve.memset(zero[:, :], 0.0).then_inc(dconst, 1)
            dve.wait_ge(consts, 12)
            dve.tensor_scalar(pads[:, :, 0], pads[:, :, 0], TT - 1, N, ALU.bitwise_and,
                              ALU.bitwise_or).then_inc(dconst, 1)
            dve.memset(pads[:, :, 1], 0).then_inc(dconst, 1)
            then(dve.tensor_copy(count[:, :], base[:, :]))

            def rsqrt(y, v, a, i=None, per=0):
                then(dve.tensor_scalar(y.bitcast(I32), v.bitcast(I32), 1, None, ALU.arith_shift_right), i, per)
                then(dve.tensor_scalar(y.bitcast(I32), y.bitcast(I32), -1, RSQRT_BITS, ALU.mult, ALU.add), i, per)
                for n in range(3):
                    then(dve.scalar_tensor_tensor(a, y, -0.5, y, ALU.mult, ALU.mult), i, per)
                    then(dve.tensor_tensor(a, a, v, ALU.mult), i, per)
                    ins = dve.scalar_tensor_tensor(y, a, 1.5, y, ALU.add, ALU.mult)
                    if n < 2:
                        then(ins, i, per)
                return ins

            def norm_group(g):
                dve.wait_ge(x_all_in[g], 16)
                for t in range(g * LNT, (g + 1) * LNT):
                    dve.bn_stats(stats[:, t, :], xall[:, t, :]).then_inc(dve_step, 1)
                steps[0] += LNT
                dve.wait_ge(dve_step, steps[0])
                for t in range(g * LNT, (g + 1) * LNT):
                    dve.bn_aggr(mv[:, t, :], stats[:, t, :]).then_inc(dve_step, 1)
                steps[0] += LNT
                dve.wait_ge(dve_step, steps[0])
                sl = slice(g * LNT, (g + 1) * LNT)
                then(dve.tensor_scalar(var[:, sl], mv[:, sl, 1], EPS, None, ALU.add))
                then(rsqrt(rstd[:, sl], var[:, sl], newton[:, sl]))
                for t in range(g * LNT, (g + 1) * LNT):
                    ins = dve.tensor_scalar(xall[:, t, :], xall[:, t, :], mv[:, t, 0:1], rstd[:, t:t + 1],
                                            ALU.subtract, ALU.mult)
                ins.then_inc(ln_ready, 1)

            def make_mask(i, k):
                n = 4 * i + k
                wait(dve, adj_in[k], 16 * (i + 1))
                wait(dve, unit_done, n - 1)
                dve.tensor_scalar(mask[k % 2], adj_sb[:, k, :], 0.0, None, ALU.is_gt).then_inc(mask_ready, 1)

            def make_low(i, k):
                wait(dve, high_ready, 4 * i + k + 1)
                dve.tensor_tensor(low[k % 2], adj_sb[:, k, :], high[k % 2],
                                  ALU.subtract).then_inc(low_ready, 1)

            def residual(i, pair, per):
                wait(dve, sums_ready, 2 * pair + 2)
                then(dve.tensor_scalar(var[:, 0:2], sums[:, :, 1, D], 1e-24, None, ALU.max), i, per)
                then(rsqrt(hscale[:, :], var[:, 0:2], newton[:, 0:2], i, per), i, per)
                for u in range(2):
                    ins = dve.scalar_tensor_tensor(num[:, u, 0:D + 1], sums[:, u, 1, 0:D + 1], hscale[:, u:u + 1],
                                                   sums[:, u, 0, 0:D + 1], ALU.mult, ALU.add)
                ins.then_inc(num_ready, 1)
                wait(dve, num_ready, pair + 1)
                then(dve.reciprocal(rec[:, :], num[:, :, D]), i, per)
                wait(dve, x_in, 16 * (pair + 1))
                wait(dve, rows_out, 32 * pair)
                for u in range(2):
                    count_step(dve.scalar_tensor_tensor(x1t[:, u, :], num[:, u, 0:D], rec[:, u:u + 1],
                                                        xt[:, u, :], ALU.mult, ALU.add))
                after(i, per)
                for u in range(2):
                    count_step(dve.bn_stats(st2[:, u, :], x1t[:, u, :]))

            def norm_rows(i, pair, per):
                after(i, per, apart=True)
                for u in range(2):
                    count_step(dve.bn_aggr(mv2[:, u, :], st2[:, u, :]))
                after(i, per)
                then(dve.tensor_scalar(var[:, 2:4], mv2[:, :, 1], EPS, None, ALU.add), i, per)
                then(rsqrt(rs2[:, :], var[:, 2:4], newton[:, 2:4], i, per), i, per)
                wait(dve, turn_ready, pair)
                for u in range(2):
                    ins = dve.tensor_scalar(xnt[:, u, :], x1t[:, u, :], mv2[:, u, 0:1], rs2[:, u:u + 1],
                                            ALU.subtract, ALU.mult)
                ins.then_inc(xn_ready, 1)

            def rows_low(pair):
                wait(dve, nh_ready, pair + 1)
                dve.tensor_tensor(xnt_hl[:, :, D:2 * D], xnt[:, :, :], xnt_hl[:, :, 0:D],
                                  ALU.subtract).then_inc(nl_ready, 1)

            entry_gate = entry[:, :, :, 1].bitcast(F32)

            def by_e(a):
                return a.unsqueeze(2).to_broadcast([P, 2, E])

            kv_b = kv[:, :].unsqueeze(1).to_broadcast([P, 2, E])

            def choose(c, pr, best, i, per):
                then(dve.tensor_reduce(best[:, :], pr[:, :, :], AX, ALU.max), i, per)
                then(dve.tensor_tensor(eq[:, :, :], pr[:, :, :], by_e(best[:, :]), ALU.is_equal), i, per)
                then(dve.tensor_tensor(eq[:, :, :], eq[:, :, :], kv_b, ALU.mult), i, per)
                then(dve.tensor_reduce(km[:, :], eq[:, :, :], AX, ALU.max), i, per)
                then(dve.tensor_tensor(oh[:, c, :, :], kv_b, by_e(km[:, :]), ALU.is_equal), i, per)

            def route(i, pair, per):
                wait(dve, logits_ready, pair + 1)
                then(dve.tensor_reduce(mx[:, :], logits, AX, ALU.max), i, per)
                dve.tensor_tensor(z[:, :, :], logits, by_e(mx[:, :]), ALU.subtract).then_inc(z_ready, 1)
                wait(dve, exp_ready, pair + 1)
                then(dve.tensor_reduce(sm[:, :], ez[:, :, :], AX, ALU.add), i, per)
                then(dve.reciprocal(sm[:, :], sm[:, :]), i, per)
                then(dve.tensor_tensor(prob[:, :, :], ez[:, :, :], by_e(sm[:, :]), ALU.mult), i, per)
                choose(0, prob, m1, i, per)
                then(dve.scalar_tensor_tensor(prob2[:, :, :], oh[:, 0, :, :], -2.0, prob[:, :, :],
                                              ALU.mult, ALU.add), i, per)
                choose(1, prob2, m2, i, per)
                dve.tensor_tensor(sel[:, :, :], oh[:, 0, :, :], oh[:, 1, :, :], ALU.add).then_inc(sel_ready, 1)
                then(dve.scalar_tensor_tensor(sm[:, :], m1[:, :], 1e-9, m2[:, :], ALU.add, ALU.add), i, per)
                then(dve.reciprocal(sm[:, :], sm[:, :]), i, per)
                for c, m in enumerate((m1, m2)):
                    count_step(dve.tensor_tensor(gates[:, c, :], m[:, :], sm[:, :], ALU.mult))

            def list_places(i, pair, per):
                wait(dve, rank_ready, pair + 1)
                then(dve.tensor_tensor(pos[:, :, :], rank, count[:, :].unsqueeze(1).to_broadcast([P, 2, E]),
                                       ALU.add), i, per)
                then(dve.tensor_tensor(count[:, :], count[:, :], total, ALU.add), i, per)
                then(dve.tensor_tensor(place[:, :, :, :], oh[:, :, :, :],
                                       pos[:, :, :].unsqueeze(1).to_broadcast([P, 2, 2, E]), ALU.mult), i, per)
                wait(dve, table_put, 64 * pair + 16)
                dve.tensor_copy(entry_gate, gates[:, :, :])
                then(dve.tensor_scalar(entry[:, :, :, 0], entry[:, :, :, 0], 2 * P, None, ALU.add), i, per)
                with nc.allow_low_precision(reason="row numbers are whole and below 2^24"):
                    dve.tensor_reduce(slots[:, :, :], place[:, :, :, :], AX, ALU.add).then_inc(slots_ready, 1)

            def body(i, per):
                make_mask(i, 0)
                make_low(i, 0)
                if at_least(i, 2):
                    route(i, i - 2, per)
                make_mask(i, 1)
                make_low(i, 1)
                residual(i, i - 1, per)
                make_mask(i, 2)
                make_low(i, 2)
                norm_rows(i, i - 1, per)
                make_mask(i, 3)
                make_low(i, 3)
                rows_low(i - 1)
                if at_least(i, 2):
                    list_places(i, i - 2, per)

            norm_group(0)
            make_mask(0, 0)
            make_low(0, 0)
            norm_group(1)
            make_mask(0, 1)
            make_low(0, 1)
            norm_group(2)
            norm_group(3)
            for k in (2, 3):
                make_mask(0, k)
                make_low(0, k)
            body(1, 0)
            per = 54
            at_loop = steps[0]
            with dve.Fori(2, NPAIR) as i:
                steps[0] = at_loop - 2 * per
                body(i, per)
                assert steps[0] == at_loop - per, (steps[0], at_loop)
            steps[0] = at_loop + per * (NPAIR - 2)
            route(NPAIR, NPAIR - 2, 0)
            residual(NPAIR, NPAIR - 1, 0)
            norm_rows(NPAIR, NPAIR - 1, 0)
            rows_low(NPAIR - 1)
            list_places(NPAIR, NPAIR - 2, 0)
            route(NPAIR, NPAIR - 1, 0)
            list_places(NPAIR, NPAIR - 1, 0)

            then(dve.tensor_tensor(nt_f[:, :], count[:, :], base[:, :], ALU.subtract))
            then(dve.tensor_scalar(nt_i[:, :], nt_f[:, :], 1.0, TT - 1.0, ALU.max, ALU.add))
            then(dve.tensor_scalar(nt_i[:, :], nt_i[:, :], TT.bit_length() - 1, None, ALU.arith_shift_right))
            then(dve.tensor_copy(nt_f[:, :], nt_i[:, :]))
            then(dve.tensor_copy(end[:, :], nt_f[:, :]))
            for e in range(1, E):
                then(dve.tensor_tensor(end[:, e:e + 1], end[:, e - 1:e], end[:, e:e + 1], ALU.add))
            then(dve.tensor_scalar(jump[:, :], nt_f[:, :], -float(TT), float(EROWS), ALU.mult, ALU.add))

            def row_b(a):
                return a[0:1, :].unsqueeze(1).to_broadcast([1, TILES, E])

            then(dve.tensor_tensor(past, ti[:, :].unsqueeze(2).to_broadcast([1, TILES, E]),
                                   row_b(end), ALU.is_ge))
            then(dve.tensor_tensor(pj, past, row_b(jump), ALU.mult))
            then(dve.tensor_reduce(te[:, :], past, AX, ALU.add))
            then(dve.tensor_reduce(tr[:, :], pj, AX, ALU.add))
            dve.tensor_scalar(tile_expert[:, :], te[:, :], float(E - 1), None, ALU.min).then_inc(tiles_ready, 1)
            dve.scalar_tensor_tensor(tile_row[:, :], ti[:, :], float(TT), tr[:, :], ALU.mult,
                                     ALU.add).then_inc(tiles_ready, 1)

            def tokens(m, b):
                j = 2 * m + b
                wait(dve, listed_in[b], 16 * (m + 1))
                wait(dve, xg_in[b], 16 * SUB * m)
                dve.tensor_copy(tok[b][:, :], listed[:, bass.ds(j, 1), :, 0].rearrange("p a s -> p (a s)")
                                ).then_inc(tok_ready, 1)

            def h_parts(m, b):
                j = 2 * m + b
                wait(dve, yp_ready, j - 1)
                for q in range(4):
                    s = slice(q * 512, (q + 1) * 512)
                    wait(dve, relu_ready, 4 * j + q + 1)
                    dve.tensor_copy(hh[b][:, s], h32[:, s]).then_inc(hh_ready, 1)
                    wait(dve, hh_ready, 4 * j + q + 1)
                    dve.tensor_tensor(hl[b][:, s], h32[:, s], hh[b][:, s], ALU.subtract).then_inc(hl_ready, 1)

            def outputs(m, b):
                j = 2 * m + b
                e = dve.value_load(tile_expert[0:1, bass.ds(j, 1)], min_val=0, max_val=E - 1)
                wait(dve, y_put, 16 * SUB * (j - 1))
                entries = listed[:, bass.ds(j, 1), :, :].rearrange("p a s w -> p (a s) w")
                dve.tensor_copy(dest[b][:, :], entries[:, :, 0])
                dve.tensor_copy(gate[b][:, :], entries[:, :, 1].bitcast(F32)).then_inc(y_step, 1)
                wait(dve, yp_ready, j + 1)
                dve.tensor_tensor(y32[b], yp[b].rearrange("p (s d) -> p s d", s=SUB),
                                  b2[:, bass.ds(e, 1), :].to_broadcast([P, SUB, D]),
                                  ALU.add).then_inc(y_step, 1)
                dve.wait_ge(y_step, 2 * (j + 1))
                for s in range(SUB):
                    ins = dve.tensor_scalar(y_out[b][:, s, :], y32[b][:, s, :], gate[b][:, s:s + 1], None, ALU.mult)
                ins.then_inc(y_ready, 1)

            def step(m, b, more_tokens=True):
                if more_tokens:
                    tokens(m + 1, b)
                h_parts(m, b)
                if not (isinstance(m, int) and 2 * m + b == 0):
                    outputs(*((m - 1, 1) if b == 0 else (m, 0)))

            tokens(0, 0)
            tokens(0, 1)
            step(0, 0)
            step(0, 1)
            step(1, 0)
            step(1, 1)
            with dve.Fori(2, LAST - 1) as m:
                step(m, 0)
                step(m, 1)
            step(LAST - 1, 0)
            step(LAST - 1, 1, more_tokens=False)
            step(LAST, 0, more_tokens=False)
            outputs(LAST, 0)

        @block.tensor
        def _(pe):
            pe.wait_ge(consts, 12)
            pe.wait_ge(small_in, 48)

            def unit(i, k):
                n, t, u, h = 4 * i + k, 2 * i + k // 2, k // 2, k % 2
                wait(pe, high_ready, n + 1)
                wait(pe, mask_ready, n + 1)
                wait(pe, low_ready, n + 1)
                if h == 0:
                    wait(pe, sums_ready, t - 1)
                for jj in range(UJ):
                    jt = h * UJ + jj
                    if isinstance(i, int) and i == 0 and k < 2 and jt % LNT == 0:
                        pe.wait_ge(cl_ready, jt // LNT + 1)
                    s = slice(jj * P, (jj + 1) * P)
                    a, m = acc[u][:, 0, :], acc[u][:, 1, :]
                    on, off = jt == 0, jt == NT - 1
                    pe.matmul(a[:, 0:D + 1], high[h][:, s], ch[:, jt, 0:D + 1], start=on, stop=False)
                    pe.matmul(a[:, 0:D], high[h][:, s], cl[:, jt, :], start=False, stop=False)
                    pe.matmul(a[:, 0:D + 1], low[h][:, s], ch[:, jt, 0:D + 1], start=False, stop=off)
                    pe.matmul(m[:, 0:D + 1], mask[h][:, s], ch[:, jt, 0:D + 1], start=on, stop=False)
                    ins = pe.matmul(m[:, 0:D], mask[h][:, s], cl[:, jt, :], start=False, stop=off)
                ins.then_inc(unit_done, 1)

            def turn(pair):
                wait(pe, xn_ready, pair + 1)
                wait(pe, xnT_ready, pair)
                for u in range(2):
                    for c in range(DC):
                        s = slice(c * P, (c + 1) * P)
                        ins = pe.transpose(turned[:, u * D + c * P:u * D + (c + 1) * P], xnt[:, u, s],
                                           ident[:, :])
                ins.then_inc(turn_ready, 1)

            def router(pair):
                wait(pe, xnT_ready, pair + 1)
                wait(pe, z_ready, pair)
                for u in range(2):
                    for c in range(DC):
                        ins = pe.matmul(logits[:, u, :], xnT[:, u * D + c * P:u * D + (c + 1) * P],
                                        rw[:, c, :], start=(c == 0), stop=(c == DC - 1))
                ins.then_inc(logits_ready, 1)

            def ranks(pair):
                wait(pe, sel_ready, pair + 1)
                pe.matmul(rank[:, 0, :], tri[:, :], sel[:, 0, :], start=True, stop=True)
                pe.matmul(rank[:, 1, :], tri[:, :], sel[:, 1, :], start=True, stop=False)
                pe.matmul(rank[:, 1, :], ones[:, :], sel[:, 0, :], start=False, stop=True)
                pe.matmul(total, ones[:, :], sel[:, 0, :], start=True, stop=False)
                pe.matmul(total, ones[:, :], sel[:, 1, :], start=False, stop=True).then_inc(rank_ready, 1)

            def body(i):
                unit(i, 0)
                if at_least(i, 2):
                    ranks(i - 2)
                unit(i, 1)
                if at_least(i, 1):
                    turn(i - 1)
                unit(i, 2)
                if at_least(i, 1):
                    router(i - 1)
                unit(i, 3)

            pairs(pe, body)
            ranks(NPAIR - 2)
            turn(NPAIR - 1)
            router(NPAIR - 1)
            ranks(NPAIR - 1)

            def part(e, which, f0, n):
                return W[:, bass.ds(e, 1), which * MATS + f0:which * MATS + f0 + n].rearrange("p a n -> p (a n)")

            def hidden(m, b):
                j = 2 * m + b
                e = pe.value_load(tile_expert[0:1, bass.ds(j, 1)], min_val=0, max_val=E - 1)
                wait(pe, w_in, 16 * e + 16)
                wait(pe, xs_ready, j + 1)
                for q in range(4):
                    wait(pe, relu_ready, 4 * j + q - 3)
                    for f in range(2 * q, 2 * q + 2):
                        o = h1[q][:, (f % 2) * TT:(f % 2 + 1) * TT]
                        for c in range(DC):
                            x_high, x_low = (xs[b][:, (h * DC + c) * TT:(h * DC + c + 1) * TT]
                                             for h in range(2))
                            w1h, w1l = (part(e, w, c * DFF + f * P, P) for w in (0, 1))
                            pe.matmul(o, w1h, x_high, start=(c == 0), stop=False)
                            pe.matmul(o, w1h, x_low, start=False, stop=False)
                            ins = pe.matmul(o, w1l, x_high, start=False, stop=(c == DC - 1))
                    ins.then_inc(h1_ready, 1)

            def x_turn(m, b):
                j = 2 * m + b
                wait(pe, xg_in[b], 16 * SUB * (m + 1))
                wait(pe, xs_ready, j - 1)
                for h in range(2):
                    for s in range(SUB):
                        for c in range(DC):
                            at = h * DC * TT + c * TT + s * P
                            ins = pe.transpose(xT[b][:, at:at + P],
                                               xg[b][:, s, h * D + c * P:h * D + (c + 1) * P], ident16[:, :])
                ins.then_inc(xt_ready, 1)

            def second(m, b):
                j = 2 * m + b
                e = pe.value_load(tile_expert[0:1, bass.ds(j, 1)], min_val=0, max_val=E - 1)
                wait(pe, y_ready, j - 1)
                for s in range(SUB):
                    for f in range(FC):
                        if s == 0 and f % 2 == 0:
                            wait(pe, hl_ready, 4 * j + f // 2 + 1)
                        fs = slice(f * TT + s * P, f * TT + (s + 1) * P)
                        o = yp[b][:, s * D:(s + 1) * D]
                        w2h, w2l = (part(e, w, f * D, D) for w in (2, 3))
                        pe.matmul(o, hh[b][:, fs], w2h, start=(f == 0), stop=False)
                        pe.matmul(o, hl[b][:, fs], w2h, start=False, stop=False)
                        ins = pe.matmul(o, hh[b][:, fs], w2l, start=False, stop=(f == FC - 1))
                ins.then_inc(yp_ready, 1)

            def step(m, b, more=True):
                hidden(m, b)
                if more:
                    x_turn(*((m, 1) if b == 0 else (m + 1, 0)))
                if not (isinstance(m, int) and 2 * m + b == 0):
                    second(*((m - 1, 1) if b == 0 else (m, 0)))

            pe.wait_ge(tiles_ready, 2)
            x_turn(0, 0)
            for m in range(2):
                step(m, 0)
                step(m, 1)
            with pe.Fori(2, LAST) as m:
                step(m, 0)
                step(m, 1)
            step(LAST, 0, more=False)
            second(LAST, 0)


def kernel(x, adj, L0_ffn_router_w, L0_ffn_w1_all, L0_ffn_b1_all, L0_ffn_w2_all, L0_ffn_b2_all):
    import numpy as np
    import concourse.bacc as bacc
    from concourse.bass_utils import run_bass_kernel_spmd as run

    a = np.asarray
    c = np.ascontiguousarray
    adj_u = c(a(adj).reshape(NPAIR, 2, P, 2, UJ, P).transpose(0, 1, 3, 5, 4, 2)).reshape(NPAIR, 4, P, UNIT)
    w1 = a(L0_ffn_w1_all).reshape(E, DFF, DC, P).transpose(3, 0, 2, 1).reshape(P, E, 1, MATS)
    w2 = a(L0_ffn_w2_all).reshape(E, D, FC, P).transpose(3, 0, 2, 1).reshape(P, E, 1, MATS)
    arrays = {
        "x": c(a(x)),
        "adj_u": adj_u,
        "w_all": c(np.concatenate([w1, w2], axis=2)).reshape(P, E * 2 * MATS),
        "b1_t": c(a(L0_ffn_b1_all).reshape(E, FC, P).transpose(2, 0, 1)).reshape(P, E * FC),
        "b2_r": c(a(L0_ffn_b2_all)).reshape(1, E, D),
        "rw_t": c(a(L0_ffn_router_w).reshape(E, DC, P).transpose(2, 1, 0)),
    }
    nc = bacc.Bacc("TRN2", target_bir_lowering=False, num_devices=1)
    args = {k: nc.dram_tensor(k, v.shape, mybir.dt.from_np(v.dtype), kind="ExternalInput").ap()
            for k, v in arrays.items()}
    out = nc.dram_tensor("out", (N + TT, D), F32, kind="ExternalOutput").ap()
    moe_gnn_kernel(nc, out=out, **args)
    r = run(nc, [arrays], core_ids=[0])
    return r.results[0]["out"][:N]
```

```python
from contextlib import ExitStack

import concourse.bass as bass
from concourse import mybir

P = 128
F32 = mybir.dt.float32
F16 = mybir.dt.float16
BF16 = mybir.dt.bfloat16
I32 = mybir.dt.int32
ALU = mybir.AluOpType
ACT = mybir.ActivationFunctionType
AX = mybir.AxisListType.X

N, D, DFF, E, K = 4096, 256, 1024, 8, 2
NT = N // P
NPAIR = NT // 2
UJ = NT // 2
UNIT = UJ * P
DC = D // P
FC = DFF // P
EPS = 1e-5
RSQRT_BITS = 0x5F3759DF
LNG = 4
LNT = NT // LNG

TT = 256
SUB = TT // P
TILES = (K * N + (TT - 1) * E) // TT
EROWS = N
ROWS = E * EROWS + (TILES - E) * TT
PADQ = ROWS // P
HE = E // 2
HM = 2 * HE
MATS = DC * DFF
EW = 4 * MATS
CH = MATS // 2
LAST = (TILES - 1) // 2

CUR_UP, ADJ_UP, W_UP, H_UP = 2.0 ** 8, 2.0 ** 4, 2.0 ** 8, 2.0 ** 4

W_LOADED = 2 * 16

CONSTS = 12

SX = 264


def moe_gnn_kernel(nc, x, adj_u, w_all, b1_t, b2_r, rw_t, out):
    with ExitStack() as ctx:
        def sb(name, shape, dt=F32):
            return ctx.enter_context(nc.sbuf_tensor(name, shape, dt))

        def sem(name):
            return ctx.enter_context(nc.semaphore(name))

        def dram(name, shape, dt=F32):
            return nc.dram_tensor(name, shape, dt).ap()

        w_split = dram("w_split", (P, E - HE, EW), F16)
        xn_rows = dram("xn_rows", (N + TT, 2 * D), F16)
        table = dram("table", (ROWS, 2), I32)

        W = sb("W", [P, E, EW], F16)
        Wf = W[:, :, :].rearrange("p e n -> p (e n)")
        lower = Wf[:, 0:HE * EW]
        upper = Wf[:, HE * EW:E * EW]
        xall = lower[:, 0:2 * NT * D].bitcast(F32).rearrange("p (t d) -> p t d", t=NT)
        adj_sb = upper[:, 0:4 * 2 * UNIT].bitcast(F32).rearrange("p (k n) -> p k n", k=4)
        at = 4 * 2 * UNIT
        parts = []
        for _ in range(6):
            parts.append(upper[:, at:at + UNIT])
            at += UNIT
        high, low, mask = parts[0:2], parts[2:4], parts[4:6]
        mask = [m.bitcast(BF16) for m in mask]
        pads = upper[:, at:at + 4 * PADQ].bitcast(I32).rearrange("p (q w) -> p q w", w=2)
        W_mats = W[:, :, :].rearrange("p e (m h n) -> p (e m) h n", m=2, h=2)

        R = sb("R", [P, NT * SX + NT * D], F16)
        ch = R[:, 0:NT * SX].rearrange("p (t d) -> p t d", t=NT)
        cl = R[:, NT * SX:].rearrange("p (t d) -> p t d", t=NT)
        Rf = R[:, :]
        at = 0

        def region(n, dt):
            nonlocal at
            words = n if dt == F16 else 2 * n
            v = Rf[:, at:at + words]
            at += words
            return v if dt == F16 else v.bitcast(dt)

        hh = [region(FC * TT, F16) for _ in range(2)]
        hl = [region(FC * TT, F16) for _ in range(2)]
        h32 = region(FC * TT, F32)
        xg = [region(SUB * 2 * D, F16).rearrange("p (s d) -> p s d", s=SUB) for _ in range(2)]
        xs = [region(2 * DC * TT, F16) for _ in range(2)]
        assert at <= NT * (SX + D)

        stage = sb("stage", [P, 2, CH])
        stage_h = sb("stage_h", [P, 2, CH], F16)
        stage_l = sb("stage_l", [P, 2, CH], F16)
        y_out = [stage[:, b, 0:SUB * D].rearrange("p (s d) -> p s d", s=SUB) for b in range(2)]
        y32 = [stage[:, b, SUB * D:2 * SUB * D].rearrange("p (s d) -> p s d", s=SUB) for b in range(2)]
        b2 = sb("b2", [P, E, D])
        b1 = sb("b1", [P, E * FC])
        rw = sb("rw", [P, DC, E])
        xt = sb("xt", [P, 2, D])
        x1t = sb("x1t", [P, 2, D])
        xnt = sb("xnt", [P, 2, D])
        xnt_hl = sb("xnt_hl", [P, 2, 2 * D], F16)
        xnT = sb("xnT", [P, 2 * D])
        sums = sb("sums", [P, 2, 2, SX])
        num = sb("num", [P, 2, SX])
        zero = sb("zero", [P, D])
        ident = sb("ident", [P, P])
        ident16 = sb("ident16", [P, P], F16)
        tri = sb("tri", [P, P], BF16)
        ones = sb("ones", [P, P], BF16)
        stats = sb("stats", [P, NT, 6])
        mv = sb("mv", [P, NT, 2])
        rstd = sb("rstd", [P, NT])
        shift = sb("shift", [P, NT])
        var = sb("var", [P, NT])
        newton = sb("newton", [P, NT])
        hscale = sb("hscale", [P, 2])
        rec = sb("rec", [P, 2])
        st2 = sb("st2", [P, 2, 6])
        mv2 = sb("mv2", [P, 2, 2])
        rs2 = sb("rs2", [P, 2])
        kv = sb("kv", [P, E])
        z = sb("z", [P, 2, E])
        ez = sb("ez", [P, 2, E])
        prob = sb("prob", [P, 2, E])
        prob2 = sb("prob2", [P, 2, E])
        eq = sb("eq", [P, 2, E])
        oh = sb("oh", [P, 2, 2, E])
        sel = sb("sel", [P, 2, E], BF16)
        mx = sb("mx", [P, 2])
        m1 = sb("m1", [P, 2])
        m2 = sb("m2", [P, 2])
        km = sb("km", [P, 2])
        sm = sb("sm", [P, 2])
        gates = sb("gates", [P, K, 2])
        count = sb("count", [P, E])
        pos = sb("pos", [P, 2, E])
        place = sb("place", [P, 2, 2, E])
        slots = sb("slots", [P, 2, 2], I32)
        entry = sb("entry", [P, 2, 2, 2], I32)
        base = sb("base", [P, E])
        nt_i = sb("nt_i", [P, E], I32)
        nt_f = sb("nt_f", [P, E])
        end = sb("end", [P, E])
        jump = sb("jump", [P, E])
        ti = sb("ti", [1, TILES])
        past, pj = (a[0:1, 0:TILES * E].rearrange("p (t e) -> p t e", e=E) for a in (
            num[:, :, :].rearrange("p u d -> p (u d)"), sums[:, :, :, :].rearrange("p u s d -> p (u s d)")))
        te = sb("te", [1, TILES])
        tr = sb("tr", [1, TILES])
        tile_expert = sb("tile_expert", [1, TILES], I32)
        tile_row = sb("tile_row", [1, TILES], I32)
        listed = sb("listed", [P, TILES, SUB, 2], I32)
        mark = sb("mark", [P, HE])
        tok = [sb(f"tok{b}", [P, SUB], I32) for b in range(2)]
        dest = [sb(f"dest{b}", [P, SUB], I32) for b in range(2)]
        gate = [sb(f"gate{b}", [P, SUB]) for b in range(2)]

        PS = ctx.enter_context(nc.psum_tensor("PS", [P, 8, 512], F32))
        acc = [PS[:, 2 * u:2 * u + 2, :] for u in range(2)]
        turned = PS[:, 4, :]
        logits = PS[:, 6, 0:2 * E].rearrange("p (u e) -> p u e", u=2)
        rank = PS[:, 7, 0:2 * E].rearrange("p (u e) -> p u e", u=2)
        total = PS[:, 7, 2 * E:3 * E]
        h1 = [PS[:, q, :] for q in range(4)]
        yp = [PS[:, 4, :], PS[:, 5, :]]
        last_yp = [PS[:, 4, :], PS[:, 6, :]]
        xT = [PS[:, 6, :].bitcast(F16), PS[:, 7, :].bitcast(F16)]

        adj_in = [sem(f"adj_in{k}") for k in range(4)]
        x_all_in = [sem(f"x_all_in{g}") for g in range(LNG)]
        x_in = sem("x_in")
        small_in = sem("small_in")
        wchunk_in = [sem(f"wchunk_in{v}") for v in range(2)]
        wsplit_out = [sem(f"wsplit_out{v}") for v in range(2)]
        rows_out = sem("rows_out")
        pads_out = sem("pads_out")
        w_in = sem("w_in")
        table_put = sem("table_put")
        listed_in = [sem(f"listed_in{b}") for b in range(2)]
        xg_in = [sem(f"xg_in{b}") for b in range(2)]
        y_put = sem("y_put")
        consts = sem("consts")
        pads_ready = sem("pads_ready")
        stats_ready = sem("stats_ready")
        ln_ready = [sem(f"ln_ready{g}") for g in range(LNG)]
        ch_ready = sem("ch_ready")
        cl_ready = sem("cl_ready")
        high_ready = sem("high_ready")
        mask_ready = sem("mask_ready")
        low_ready = sem("low_ready")
        unit_done = sem("unit_done")
        sums_ready = sem("sums_ready")
        num_ready = sem("num_ready")
        xn_ready = sem("xn_ready")
        rows_high_ready = sem("rows_high_ready")
        rows_low_ready = sem("rows_low_ready")
        turn_ready = sem("turn_ready")
        xnT_ready = sem("xnT_ready")
        logits_ready = sem("logits_ready")
        z_ready = sem("z_ready")
        exp_ready = sem("exp_ready")
        sel_ready = sem("sel_ready")
        rank_ready = sem("rank_ready")
        slots_ready = sem("slots_ready")
        wscaled_ready = sem("wscaled_ready")
        whigh_ready = sem("whigh_ready")
        wlow_ready = sem("wlow_ready")
        tiles_ready = sem("tiles_ready")
        tok_ready = sem("tok_ready")
        xt_ready = sem("xt_ready")
        xs_ready = sem("xs_ready")
        b1_ready = sem("b1_ready")
        h1_ready = sem("h1_ready")
        relu_ready = sem("relu_ready")
        hh_ready = sem("hh_ready")
        hl_ready = sem("hl_ready")
        yp_ready = sem("yp_ready")
        y_step = sem("y_step")
        y_ready = sem("y_ready")
        dve_step = sem("dve_step")

        def wait(eng, s, value):
            if isinstance(value, int) and value <= 0:
                return
            eng.wait_ge(s, value)

        def waits_apart(eng, *pairs):
            pairs = [(s, v if isinstance(v, int) else eng.to_reg(v)) for s, v in pairs]
            if not all(isinstance(v, int) for _, v in pairs):
                eng.wait_ge(consts, CONSTS)
            for s, v in pairs:
                wait(eng, s, v)

        def pairs(eng, body, *phases):
            body(0)
            body(1)
            for first, last in phases or [(2, NPAIR)]:
                with eng.Fori(first, last) as i:
                    body(i)

        def at_least(i, n):
            return not isinstance(i, int) or i >= n

        block = ctx.enter_context(nc.Block())

        @block.sync
        def _(sp):
            def load_unit(i, k):
                sp.dma_start(adj_sb[:, k, :],
                             adj_u[bass.ds(i, 1), k].rearrange("a p n -> p (a n)")).then_inc(adj_in[k], 16)

            def load_x(i):
                sp.dma_start(xt[:, :, :], x[bass.ds(i * 2 * P, 2 * P), :].rearrange("(u p) d -> p u d", u=2)
                             ).then_inc(x_in, 16)

            def load_w(c, v):
                sp.dma_start(stage[:, v, :], w_all[:, bass.ds(c * CH, CH)]).then_inc(wchunk_in[v], 16)

            def store_rows(i):
                rows = bass.ds(i * 2 * P, 2 * P)
                wait(sp, rows_low_ready, i + 1)
                sp.dma_start(xn_rows[rows, :].rearrange("(u p) d -> p u d", u=2),
                             xnt_hl[:, :, :]).then_inc(rows_out, 16)
                sp.dma_start(out[rows, :].rearrange("(u p) d -> p u d", u=2),
                             x1t[:, :, :]).then_inc(rows_out, 16)

            x_v = x.rearrange("(t p) d -> p t d", p=P)
            for g in range(LNG):
                sp.dma_start(xall[:, g * LNT:(g + 1) * LNT, :],
                             x_v[:, g * LNT:(g + 1) * LNT, :]).then_inc(x_all_in[g], 16)
                if g == 1:
                    load_unit(0, 0)
            for k in range(1, 4):
                load_unit(0, k)
            sp.dma_start(rw[:, :, :], rw_t).then_inc(small_in, 16)
            sp.dma_start(b1[:, :], b1_t).then_inc(small_in, 16)
            sp.dma_start(b2[:, :, :], b2_r.to_broadcast([P, E, D])).then_inc(small_in, 16)
            load_x(0)
            for v in range(2):
                load_w(v, v)
            sp.wait_ge(pads_ready, 3)
            for s in range(SUB):
                rows = slice(N + s * P, N + (s + 1) * P)
                sp.dma_start(out[rows, :], zero[:, :]).then_inc(pads_out, 16)
                sp.dma_start(xn_rows[rows, :], zero[:, :].bitcast(F16)).then_inc(pads_out, 16)

            def store_split(i, v):
                to = w_split.rearrange("p e (m h n) -> p (e m) h n", m=2, h=2)
                for h, part in enumerate((stage_h, stage_l)):
                    sp.dma_start(to[:, bass.ds(i - HM, 1), h, v * CH:(v + 1) * CH].rearrange("p a n -> p (a n)"),
                                 part[:, v, :]).then_inc(wsplit_out[v], 16)

            def load_expert(e):
                for v in range(2):
                    sp.wait_ge(wsplit_out[v], 32 * (2 * (e - HE) + 2))
                for half in range(2):
                    if not (e == HE and half == 0):
                        sp.wait_ge(w_in, W_LOADED * e + 16 * half)
                    part = slice(half * EW // 2, (half + 1) * EW // 2)
                    sp.dma_start(W[:, e, part], w_split[:, e - HE, part]).then_inc(w_in, 16)

            def body(i, more=True, upper_half=False):
                for k in range(4):
                    if more:
                        wait(sp, low_ready, 4 * i + k + 1)
                        load_unit(i + 1, k)
                    if k == 3 and at_least(i, 1):
                        store_rows(i - 1)
                        load_x(i)
                    if not more and k in (1, 3):
                        wait(sp, low_ready, 4 * i + k + 1)
                        load_expert(HE + k // 2)
                    if k in (1, 3):
                        v = k // 2
                        wait(sp, wlow_ready, 2 * i + v + 1)
                        if upper_half:
                            store_split(i, v)
                        if more:
                            load_w(2 * (i + 1) + v, v)

            body(0)
            body(1)
            with sp.Fori(2, HM) as i:
                body(i)
            with sp.Fori(HM, NPAIR - 1) as i:
                body(i, upper_half=True)
            sp.wait_ge(w_in, W_LOADED * HE)
            body(NPAIR - 1, more=False, upper_half=True)

            def load_list(m, b):
                j = 2 * m + b
                row = sp.value_load(tile_row[0:1, bass.ds(j, 1)], min_val=0, max_val=ROWS - TT)
                wait(sp, listed_in[b], 16 * m)
                sp.dma_start(listed[:, bass.ds(j, 1), :, :].rearrange("p a s w -> p (a s w)"),
                             table[bass.ds(row, TT), :].rearrange("(p s) w -> p (s w)", s=SUB)
                             ).then_inc(listed_in[b], 16)

            store_rows(NPAIR - 1)
            sp.wait_ge(tiles_ready, 2)
            sp.wait_ge(table_put, 16 * (4 * NPAIR + 1))
            load_list(0, 0)
            load_list(0, 1)
            with sp.Fori(1, LAST) as m:
                load_list(m, 0)
                load_list(m, 1)
            load_list(LAST, 0)
            sp.wait_ge(unit_done, 2 * NT)
            for e in range(HE + 2, E):
                load_expert(e)
            sp.wait_ge(y_put, 16 * SUB * TILES)

        @block.gpsimd
        def _(pool):
            pool.memset(ident[:, :], 0.0).then_inc(consts, 1)
            pool.memset(tri[:, :], 1.0).then_inc(consts, 1)
            pool.memset(ones[:, :], 1.0).then_inc(consts, 1)
            pool.memset(ch[:, :, D:D + 2], CUR_UP).then_inc(consts, 1)
            pool.wait_ge(consts, 2)
            pool.affine_select(out=ident[:, :], in_=ident[:, :], compare_op=ALU.not_equal, fill=1.0,
                               base=0, pattern=[[-1, P]], channel_multiplier=1).then_inc(consts, 1)
            pool.affine_select(out=tri[:, :], in_=tri[:, :], compare_op=ALU.is_gt, fill=0.0,
                               base=0, pattern=[[1, P]], channel_multiplier=-1).then_inc(consts, 1)
            pool.iota(pads[:, :, 0], [[1, PADQ]], base=0, channel_multiplier=PADQ).then_inc(consts, 1)
            pool.iota(entry[:, :, :, 0], [[0, 2], [P, 2]], base=-2 * P, channel_multiplier=1).then_inc(consts, 1)
            pool.iota(kv[:, :], [[-1, E]], base=E, channel_multiplier=0,
                      allow_small_or_imprecise_dtypes=True).then_inc(consts, 1)
            pool.iota(base[:, :], [[EROWS, E]], base=0, channel_multiplier=0,
                      allow_small_or_imprecise_dtypes=True).then_inc(consts, 1)
            pool.iota(ti[:, :], [[1, TILES]], base=0, channel_multiplier=0,
                      allow_small_or_imprecise_dtypes=True).then_inc(consts, 1)

            pool.wait_ge(consts, 11)
            pool.tensor_copy(ident16[:, :], ident[:, :]).then_inc(consts, 1)

            pool.wait_ge(pads_ready, 3)
            pool.dma_start(table.rearrange("(p q) w -> p q w", p=P), pads[:, :, :]).then_inc(table_put, 16)

            for g in range(LNG - 1):
                pool.wait_ge(ch_ready, g + 1)
                sl = slice(g * LNT, (g + 1) * LNT)
                pool.tensor_tensor(cl[:, sl, :], xall[:, sl, :], ch[:, sl, 0:D],
                                   ALU.subtract).then_inc(cl_ready, 1)

            def split(i, v, upper_half):
                if upper_half:
                    parts = stage_h[:, v, :], stage_l[:, v, :]
                else:
                    parts = (W_mats[:, bass.ds(i, 1), h, v * CH:(v + 1) * CH].rearrange("p a n -> p (a n)")
                             for h in range(2))
                w_high, w_low = parts
                if upper_half and not (isinstance(i, int) and i == HM):
                    waits_apart(pool, (wscaled_ready, 2 * i + v + 1), (wsplit_out[v], 32 * (i - HM)))
                else:
                    waits_apart(pool, (wscaled_ready, 2 * i + v + 1))
                pool.tensor_copy(w_high, stage[:, v, :]).then_inc(whigh_ready, 1)
                waits_apart(pool, (whigh_ready, 2 * i + v + 1))
                pool.tensor_tensor(w_low, stage[:, v, :], w_high, ALU.subtract).then_inc(wlow_ready, 1)

            def scatter(i):
                waits_apart(pool, (slots_ready, i + 1))
                for c in range(2):
                    for u in range(2):
                        waits_apart(pool, (table_put, 16 * (4 * i + 2 * c + u + 1)))
                        pool.indirect_dma_start(
                            table, bass.IndirectOffsetOnAxis(slots[:, c, u:u + 1], 0),
                            entry[:, c, u, :], None).then_inc(table_put, 16)

            def body(i, upper_half=False):
                split(i, 0, upper_half)
                if at_least(i, 2):
                    scatter(i - 2)
                split(i, 1, upper_half)

            pool.wait_ge(cl_ready, LNG)
            pool.wait_ge(ch_ready, LNG)
            body(0)
            body(1)
            with pool.Fori(2, HM) as i:
                body(i)
            pool.wait_ge(wlow_ready, 2 * HM)
            for e in range(HE):
                pool.memset(mark[:, e:e + 1], 0.0).then_inc(w_in, W_LOADED)
            body(HM, upper_half=True)
            with pool.Fori(HM + 1, NPAIR) as i:
                body(i, upper_half=True)
            scatter(NPAIR - 2)
            scatter(NPAIR - 1)

            def gather(m, b):
                j = 2 * m + b
                waits_apart(pool, (tok_ready, j + 1), (xt_ready, j - 1))
                if isinstance(j, int) and j == 0:
                    pool.wait_ge(rows_out, 32 * NPAIR)
                    pool.wait_ge(pads_out, 16 * 2 * SUB)
                for s in range(SUB):
                    pool.indirect_dma_start(xg[b][:, s, :], None, xn_rows,
                                            bass.IndirectOffsetOnAxis(tok[b][:, s:s + 1], 0)
                                            ).then_inc(xg_in[b], 16)

            def put(m, b):
                j = 2 * m + b
                waits_apart(pool, (y_ready, j + 1))
                for s in range(SUB):
                    if isinstance(m, int) and m == LAST:
                        pool.wait_ge(y_ready, j + 1 + s)
                    waits_apart(pool, (y_put, 16 * (SUB * j + s)))
                    pool.indirect_dma_start(out, bass.IndirectOffsetOnAxis(dest[b][:, s:s + 1], 0),
                                            y_out[b][:, s, :], None, compute_op=ALU.add
                                            ).then_inc(y_put, 16)

            def step(m):
                put(m - 2, 0)
                gather(m, 0)
                put(m - 2, 1)
                gather(m, 1)

            for m in range(2):
                gather(m, 0)
                gather(m, 1)
            step(2)
            with pool.Fori(3, LAST) as m:
                step(m)
            put(LAST - 2, 0)
            gather(LAST, 0)
            put(LAST - 2, 1)
            put(LAST - 1, 0)
            put(LAST - 1, 1)
            put(LAST, 0)

        @block.scalar
        def _(act):
            def norm(g):
                act.wait_ge(stats_ready, g // 2 + 1)
                for t in range(g * LNT, (g + 1) * LNT):
                    ins = act.activation(xall[:, t, :], xall[:, t, :], ACT.Identity, bias=shift[:, t:t + 1],
                                         scale=rstd[:, t:t + 1])
                ins.then_inc(ln_ready[g], 1)

            def cur_high(g):
                act.wait_ge(ln_ready[g], 1)
                sl = slice(g * LNT, (g + 1) * LNT)
                act.activation(ch[:, sl, 0:D], xall[:, sl, :], ACT.Copy).then_inc(ch_ready, 1)

            def make_high(i, k):
                n = 4 * i + k
                wait(act, adj_in[k], 16 * (i + 1))
                wait(act, unit_done, n - 1)
                act.activation(high[k % 2], adj_sb[:, k, :], ACT.Copy, scale=ADJ_UP).then_inc(high_ready, 1)

            def scale_weights(i, v):
                wait(act, wchunk_in[v], 16 * (i + 1))
                act.activation(stage[:, v, :], stage[:, v, :], ACT.Copy, scale=W_UP).then_inc(wscaled_ready, 1)

            def copy_sums(i, u):
                wait(act, unit_done, 4 * i + 2 * u + 2)
                wait(act, num_ready, i)
                act.activation(sums[:, u, :, 0:D + 1], acc[u][:, :, 0:D + 1], ACT.Copy).then_inc(sums_ready, 1)

            def rows_high(i):
                wait(act, xn_ready, i + 1)
                wait(act, rows_out, 32 * i)
                act.activation(xnt_hl[:, :, 0:D], xnt[:, :, :], ACT.Copy, scale=CUR_UP).then_inc(rows_high_ready, 1)

            def copy_turned(i):
                wait(act, turn_ready, i + 1)
                wait(act, logits_ready, i)
                act.activation(xnT[:, :], turned, ACT.Copy).then_inc(xnT_ready, 1)

            def exps(i):
                wait(act, z_ready, i + 1)
                act.activation(ez[:, :, :], z[:, :, :], ACT.Exp).then_inc(exp_ready, 1)

            def body(i):
                first = not at_least(i, 1)
                if first:
                    norm(0)
                    cur_high(0)
                make_high(i, 0)
                if at_least(i, 2):
                    exps(i - 2)
                if first:
                    cur_high(1)
                else:
                    copy_sums(i - 1, 1)
                make_high(i, 1)
                if first:
                    norm(2)
                    cur_high(2)
                    cur_high(3)
                scale_weights(i, 0)
                make_high(i, 2)
                if not first:
                    rows_high(i - 1)
                copy_sums(i, 0)
                make_high(i, 3)
                if not first:
                    copy_turned(i - 1)
                scale_weights(i, 1)

            pairs(act, body)
            exps(NPAIR - 2)
            copy_sums(NPAIR - 1, 1)
            rows_high(NPAIR - 1)
            copy_turned(NPAIR - 1)
            exps(NPAIR - 1)

            def hidden(m, b):
                j = 2 * m + b
                e = act.value_load(tile_expert[0:1, bass.ds(j, 1)], min_val=0, max_val=E - 1)
                for q in range(4):
                    wait(act, h1_ready, 4 * j + q + 1)
                    wait(act, hl_ready, 4 * j + q - 3)
                    for f in range(2 * q, 2 * q + 2):
                        ins = act.activation(h32[:, f * TT:(f + 1) * TT],
                                             h1[q][:, (f % 2) * TT:(f % 2 + 1) * TT], ACT.Relu,
                                             scale=H_UP / (W_UP * CUR_UP), bias=b1[:, bass.ds(e * FC + f, 1)])
                    ins.then_inc(relu_ready, 1)

            def x_parts(m, b):
                j = 2 * m + b
                wait(act, xt_ready, j + 1)
                wait(act, h1_ready, 4 * (j - 1))
                act.activation(xs[b], xT[b], ACT.Copy).then_inc(xs_ready, 1)

            act.wait_ge(small_in, 48)
            act.activation(b1[:, :], b1[:, :], ACT.Copy, scale=H_UP).then_inc(b1_ready, 1)
            act.wait_ge(b1_ready, 1)
            act.wait_ge(tiles_ready, 2)
            x_parts(0, 0)
            hidden(0, 0)
            x_parts(0, 1)
            with act.Fori(0, LAST - 1) as m:
                hidden(m, 1)
                x_parts(m + 1, 0)
                hidden(m + 1, 0)
                x_parts(m + 1, 1)
            hidden(LAST - 1, 1)
            x_parts(LAST, 0)
            hidden(LAST, 0)

        PAIR_STEPS = 17 + 14 + 19 + 4

        @block.vector
        def _(dve):
            steps = [0]

            def count_step(ins):
                steps[0] += 1
                ins.then_inc(dve_step, 1)

            def then(ins, i=None, per=0, apart=False):
                count_step(ins)
                after(i, per, apart)

            def after(i=None, per=0, apart=False):
                value = steps[0] if i is None else steps[0] + i * per
                if apart:
                    waits_apart(dve, (dve_step, value))
                else:
                    dve.wait_ge(dve_step, value)

            dve.memset(zero[:, :], 0.0).then_inc(pads_ready, 1)
            dve.wait_ge(consts, CONSTS)
            dve.tensor_scalar(pads[:, :, 0], pads[:, :, 0], TT - 1, N, ALU.bitwise_and,
                              ALU.bitwise_or).then_inc(pads_ready, 1)
            dve.memset(pads[:, :, 1], 0).then_inc(pads_ready, 1)
            then(dve.tensor_copy(count[:, :], base[:, :]))

            def rsqrt(y, v, a, i=None, per=0):
                then(dve.tensor_scalar(y.bitcast(I32), v.bitcast(I32), 1, None, ALU.arith_shift_right), i, per)
                then(dve.tensor_scalar(y.bitcast(I32), y.bitcast(I32), -1, RSQRT_BITS, ALU.mult, ALU.add), i, per)
                for n in range(3):
                    then(dve.scalar_tensor_tensor(a, y, -0.5, y, ALU.mult, ALU.mult), i, per)
                    then(dve.tensor_tensor(a, a, v, ALU.mult), i, per)
                    ins = dve.scalar_tensor_tensor(y, a, 1.5, y, ALU.add, ALU.mult)
                    if n < 2:
                        then(ins, i, per)
                return ins

            def group_stats(g):
                dve.wait_ge(x_all_in[g], 16)
                for t in range(g * LNT, (g + 1) * LNT):
                    count_step(dve.bn_stats(stats[:, t, :], xall[:, t, :]))

            def group_scales(half):
                tiles = slice(2 * half * LNT, 2 * (half + 1) * LNT)
                after()
                for t in range(tiles.start, tiles.stop):
                    count_step(dve.bn_aggr(mv[:, t, :], stats[:, t, :]))
                after()
                then(dve.tensor_scalar(var[:, tiles], mv[:, tiles, 1], EPS, None, ALU.add))
                then(rsqrt(rstd[:, tiles], var[:, tiles], newton[:, tiles]))
                then(dve.tensor_scalar(rstd[:, tiles], rstd[:, tiles], CUR_UP, None, ALU.mult))
                dve.scalar_tensor_tensor(shift[:, tiles], mv[:, tiles, 0], -1.0, rstd[:, tiles], ALU.mult,
                                         ALU.mult).then_inc(stats_ready, 1)

            def make_mask(i, k):
                n = 4 * i + k
                wait(dve, adj_in[k], 16 * (i + 1))
                wait(dve, unit_done, n - 1)
                dve.tensor_scalar(mask[k % 2], adj_sb[:, k, :], 0.0, None, ALU.is_gt).then_inc(mask_ready, 1)

            def make_low(i, k):
                wait(dve, high_ready, 4 * i + k + 1)
                dve.scalar_tensor_tensor(low[k % 2], adj_sb[:, k, :], ADJ_UP, high[k % 2], ALU.mult,
                                         ALU.subtract).then_inc(low_ready, 1)

            def residual(i, pair, per):
                wait(dve, sums_ready, 2 * pair + 2)
                then(dve.tensor_scalar(var[:, 0:2], sums[:, :, 1, D], 1 / (CUR_UP * ADJ_UP ** 2), 1e-24,
                                       ALU.mult, ALU.max), i, per)
                then(rsqrt(hscale[:, :], var[:, 0:2], newton[:, 0:2], i, per), i, per)
                for u in range(2):
                    ins = dve.scalar_tensor_tensor(num[:, u, 0:D + 1], sums[:, u, 1, 0:D + 1], hscale[:, u:u + 1],
                                                   sums[:, u, 0, 0:D + 1], ALU.mult, ALU.add)
                ins.then_inc(num_ready, 1)
                wait(dve, num_ready, pair + 1)
                then(dve.reciprocal(rec[:, :], num[:, :, D]), i, per)
                wait(dve, x_in, 16 * (pair + 1))
                wait(dve, rows_out, 32 * pair)
                for u in range(2):
                    count_step(dve.scalar_tensor_tensor(x1t[:, u, :], num[:, u, 0:D], rec[:, u:u + 1],
                                                        xt[:, u, :], ALU.mult, ALU.add))
                after(i, per)
                for u in range(2):
                    count_step(dve.bn_stats(st2[:, u, :], x1t[:, u, :]))

            def norm_rows(i, pair, per):
                after(i, per, apart=True)
                for u in range(2):
                    count_step(dve.bn_aggr(mv2[:, u, :], st2[:, u, :]))
                after(i, per)
                then(dve.tensor_scalar(var[:, 2:4], mv2[:, :, 1], EPS, None, ALU.add), i, per)
                then(rsqrt(rs2[:, :], var[:, 2:4], newton[:, 2:4], i, per), i, per)
                wait(dve, turn_ready, pair)
                for u in range(2):
                    ins = dve.tensor_scalar(xnt[:, u, :], x1t[:, u, :], mv2[:, u, 0:1], rs2[:, u:u + 1],
                                            ALU.subtract, ALU.mult)
                ins.then_inc(xn_ready, 1)

            def rows_low(pair):
                wait(dve, rows_high_ready, pair + 1)
                dve.scalar_tensor_tensor(xnt_hl[:, :, D:2 * D], xnt[:, :, :], CUR_UP, xnt_hl[:, :, 0:D],
                                         ALU.mult, ALU.subtract).then_inc(rows_low_ready, 1)

            entry_gate = entry[:, :, :, 1].bitcast(F32)

            def by_e(a):
                return a.unsqueeze(2).to_broadcast([P, 2, E])

            kv_b = kv[:, :].unsqueeze(1).to_broadcast([P, 2, E])

            def choose(c, pr, best, i, per):
                then(dve.tensor_reduce(best[:, :], pr[:, :, :], AX, ALU.max), i, per)
                then(dve.tensor_tensor(eq[:, :, :], pr[:, :, :], by_e(best[:, :]), ALU.is_equal), i, per)
                then(dve.tensor_tensor(eq[:, :, :], eq[:, :, :], kv_b, ALU.mult), i, per)
                then(dve.tensor_reduce(km[:, :], eq[:, :, :], AX, ALU.max), i, per)
                then(dve.tensor_tensor(oh[:, c, :, :], kv_b, by_e(km[:, :]), ALU.is_equal), i, per)

            def route(i, pair, per):
                wait(dve, logits_ready, pair + 1)
                then(dve.tensor_reduce(mx[:, :], logits, AX, ALU.max), i, per)
                dve.tensor_tensor(z[:, :, :], logits, by_e(mx[:, :]), ALU.subtract).then_inc(z_ready, 1)
                wait(dve, exp_ready, pair + 1)
                then(dve.tensor_reduce(sm[:, :], ez[:, :, :], AX, ALU.add), i, per)
                then(dve.reciprocal(sm[:, :], sm[:, :]), i, per)
                then(dve.tensor_tensor(prob[:, :, :], ez[:, :, :], by_e(sm[:, :]), ALU.mult), i, per)
                choose(0, prob, m1, i, per)
                then(dve.scalar_tensor_tensor(prob2[:, :, :], oh[:, 0, :, :], -2.0, prob[:, :, :],
                                              ALU.mult, ALU.add), i, per)
                choose(1, prob2, m2, i, per)
                dve.tensor_tensor(sel[:, :, :], oh[:, 0, :, :], oh[:, 1, :, :], ALU.add).then_inc(sel_ready, 1)
                then(dve.scalar_tensor_tensor(sm[:, :], m1[:, :], 1e-9, m2[:, :], ALU.add, ALU.add), i, per)
                then(dve.reciprocal(sm[:, :], sm[:, :]), i, per)
                for c, m in enumerate((m1, m2)):
                    count_step(dve.tensor_tensor(gates[:, c, :], m[:, :], sm[:, :], ALU.mult))

            def list_places(i, pair, per):
                wait(dve, rank_ready, pair + 1)
                then(dve.tensor_tensor(pos[:, :, :], rank, count[:, :].unsqueeze(1).to_broadcast([P, 2, E]),
                                       ALU.add), i, per)
                then(dve.tensor_tensor(count[:, :], count[:, :], total, ALU.add), i, per)
                then(dve.tensor_tensor(place[:, :, :, :], oh[:, :, :, :],
                                       pos[:, :, :].unsqueeze(1).to_broadcast([P, 2, 2, E]), ALU.mult), i, per)
                wait(dve, table_put, 64 * pair + 16)
                dve.tensor_copy(entry_gate, gates[:, :, :])
                then(dve.tensor_scalar(entry[:, :, :, 0], entry[:, :, :, 0], 2 * P, None, ALU.add), i, per)
                with nc.allow_low_precision(reason="row numbers are whole and below 2^24"):
                    dve.tensor_reduce(slots[:, :, :], place[:, :, :, :], AX, ALU.add).then_inc(slots_ready, 1)

            def body(i, per):
                make_mask(i, 0)
                make_low(i, 0)
                if at_least(i, 2):
                    route(i, i - 2, per)
                make_mask(i, 1)
                make_low(i, 1)
                residual(i, i - 1, per)
                make_mask(i, 2)
                make_low(i, 2)
                norm_rows(i, i - 1, per)
                make_mask(i, 3)
                make_low(i, 3)
                rows_low(i - 1)
                if at_least(i, 2):
                    list_places(i, i - 2, per)

            def norm(g):
                dve.wait_ge(stats_ready, g // 2 + 1)
                for t in range(g * LNT, (g + 1) * LNT):
                    ins = dve.tensor_scalar(xall[:, t, :], xall[:, t, :], rstd[:, t:t + 1], shift[:, t:t + 1],
                                            ALU.mult, ALU.add)
                ins.then_inc(ln_ready[g], 1)

            group_stats(0)
            group_stats(1)
            group_scales(0)
            norm(1)
            make_mask(0, 0)
            group_stats(2)
            group_stats(3)
            group_scales(1)
            make_low(0, 0)
            norm(3)
            make_mask(0, 1)
            make_low(0, 1)
            sl = slice((LNG - 1) * LNT, LNG * LNT)
            dve.wait_ge(ch_ready, LNG)
            dve.wait_ge(cl_ready, LNG - 1)
            dve.tensor_tensor(cl[:, sl, :], xall[:, sl, :], ch[:, sl, 0:D], ALU.subtract).then_inc(cl_ready, 1)
            for k in (2, 3):
                make_mask(0, k)
                make_low(0, k)
            body(1, 0)
            per = PAIR_STEPS
            at_loop = steps[0]
            with dve.Fori(2, NPAIR) as i:
                steps[0] = at_loop - 2 * per
                body(i, per)
                assert steps[0] == at_loop - per, (steps[0], at_loop)
            steps[0] = at_loop + per * (NPAIR - 2)
            route(NPAIR, NPAIR - 2, 0)
            residual(NPAIR, NPAIR - 1, 0)
            list_places(NPAIR, NPAIR - 2, 0)
            norm_rows(NPAIR, NPAIR - 1, 0)
            rows_low(NPAIR - 1)
            route(NPAIR, NPAIR - 1, 0)
            list_places(NPAIR, NPAIR - 1, 0)

            then(dve.tensor_tensor(nt_f[:, :], count[:, :], base[:, :], ALU.subtract))
            then(dve.tensor_scalar(nt_i[:, :], nt_f[:, :], 1.0, TT - 1.0, ALU.max, ALU.add))
            then(dve.tensor_scalar(nt_i[:, :], nt_i[:, :], TT.bit_length() - 1, None, ALU.arith_shift_right))
            then(dve.tensor_copy(nt_f[:, :], nt_i[:, :]))
            then(dve.tensor_copy(end[:, :], nt_f[:, :]))
            for e in range(1, E):
                then(dve.tensor_tensor(end[:, e:e + 1], end[:, e - 1:e], end[:, e:e + 1], ALU.add))
            then(dve.tensor_scalar(jump[:, :], nt_f[:, :], -float(TT), float(EROWS), ALU.mult, ALU.add))

            def row_b(a):
                return a[0:1, :].unsqueeze(1).to_broadcast([1, TILES, E])

            then(dve.tensor_tensor(past, ti[:, :].unsqueeze(2).to_broadcast([1, TILES, E]),
                                   row_b(end), ALU.is_ge))
            then(dve.tensor_tensor(pj, past, row_b(jump), ALU.mult))
            then(dve.tensor_reduce(te[:, :], past, AX, ALU.add))
            then(dve.tensor_reduce(tr[:, :], pj, AX, ALU.add))
            dve.tensor_scalar(tile_expert[:, :], te[:, :], float(E - 1), None, ALU.min).then_inc(tiles_ready, 1)
            dve.scalar_tensor_tensor(tile_row[:, :], ti[:, :], float(TT), tr[:, :], ALU.mult,
                                     ALU.add).then_inc(tiles_ready, 1)

            def tokens(m, b):
                j = 2 * m + b
                wait(dve, listed_in[b], 16 * (m + 1))
                wait(dve, xg_in[b], 16 * SUB * m)
                dve.tensor_copy(tok[b][:, :], listed[:, bass.ds(j, 1), :, 0].rearrange("p a s -> p (a s)")
                                ).then_inc(tok_ready, 1)

            def h_parts(m, b):
                j = 2 * m + b
                wait(dve, yp_ready, j - 1)
                for q in range(4):
                    s = slice(q * 512, (q + 1) * 512)
                    wait(dve, relu_ready, 4 * j + q + 1)
                    dve.tensor_copy(hh[b][:, s], h32[:, s]).then_inc(hh_ready, 1)
                    wait(dve, hh_ready, 4 * j + q + 1)
                    dve.tensor_tensor(hl[b][:, s], h32[:, s], hh[b][:, s], ALU.subtract).then_inc(hl_ready, 1)

            def outputs(m, b, banks=None):
                j = 2 * m + b
                e = dve.value_load(tile_expert[0:1, bass.ds(j, 1)], min_val=0, max_val=E - 1)
                wait(dve, y_put, 16 * SUB * (j - 1))
                entries = listed[:, bass.ds(j, 1), :, :].rearrange("p a s w -> p (a s) w")
                dve.tensor_copy(dest[b][:, :], entries[:, :, 0])
                dve.tensor_copy(gate[b][:, :], entries[:, :, 1].bitcast(F32)).then_inc(y_step, 1)
                if banks:
                    dve.wait_ge(y_step, 2 * j + 1)
                    for s in range(SUB):
                        dve.wait_ge(yp_ready, j + 1 + s)
                        dve.scalar_tensor_tensor(y32[b][:, s, :], banks[s][:, s * D:(s + 1) * D],
                                                 1 / (H_UP * W_UP), b2[:, bass.ds(e, 1), :].rearrange(
                                                     "p a d -> p (a d)"), ALU.mult, ALU.add).then_inc(y_step, 1)
                        dve.wait_ge(y_step, 2 * j + 2 + s)
                        dve.tensor_scalar(y_out[b][:, s, :], y32[b][:, s, :], gate[b][:, s:s + 1], None,
                                          ALU.mult).then_inc(y_ready, 1)
                    return
                wait(dve, yp_ready, j + 1)
                dve.scalar_tensor_tensor(y32[b], yp[b].rearrange("p (s d) -> p s d", s=SUB),
                                         1 / (H_UP * W_UP), b2[:, bass.ds(e, 1), :].to_broadcast([P, SUB, D]),
                                         ALU.mult, ALU.add).then_inc(y_step, 1)
                dve.wait_ge(y_step, 2 * (j + 1))
                for s in range(SUB):
                    ins = dve.tensor_scalar(y_out[b][:, s, :], y32[b][:, s, :], gate[b][:, s:s + 1], None, ALU.mult)
                ins.then_inc(y_ready, 1)

            def step(m, b, more_tokens=True):
                if more_tokens:
                    tokens(m + 1, b)
                h_parts(m, b)
                if not (isinstance(m, int) and 2 * m + b == 0):
                    outputs(*((m - 1, 1) if b == 0 else (m, 0)))

            tokens(0, 0)
            tokens(0, 1)
            step(0, 0)
            step(0, 1)
            step(1, 0)
            step(1, 1)
            with dve.Fori(2, LAST - 1) as m:
                step(m, 0)
                step(m, 1)
            step(LAST - 1, 0)
            step(LAST - 1, 1, more_tokens=False)
            step(LAST, 0, more_tokens=False)
            outputs(LAST, 0, banks=last_yp)

        @block.tensor
        def _(pe):
            cl_pair = R[:, NT * SX:NT * SX + 2 * D]

            def warm(count):
                for _ in range(count):
                    pe.matmul(turned, ident16[:, :], cl_pair, start=True, stop=True)

            pe.wait_ge(consts, CONSTS)
            pe.wait_ge(cl_ready, 1)
            warm(12)

            def unit(i, k):
                n, t, u, h = 4 * i + k, 2 * i + k // 2, k // 2, k % 2
                wait(pe, high_ready, n + 1)
                wait(pe, mask_ready, n + 1)
                wait(pe, low_ready, n + 1)
                if h == 0:
                    wait(pe, sums_ready, t - 1)
                for jj in range(UJ):
                    jt = h * UJ + jj
                    if isinstance(i, int) and i == 0 and k < 2 and jt % LNT == 0:
                        pe.wait_ge(cl_ready, jt // LNT + 1)
                    s = slice(jj * P, (jj + 1) * P)
                    a, m = acc[u][:, 0, :], acc[u][:, 1, :]
                    on, off = jt == 0, jt == NT - 1
                    pe.matmul(a[:, 0:D + 1], high[h][:, s], ch[:, jt, 0:D + 1], start=on, stop=False)
                    pe.matmul(a[:, 0:D], high[h][:, s], cl[:, jt, :], start=False, stop=False)
                    pe.matmul(a[:, 0:D + 1], low[h][:, s], ch[:, jt, 0:D + 1], start=False, stop=off)
                    pe.matmul(m[:, 0:D + 1], mask[h][:, s], ch[:, jt, 0:D + 1], start=on, stop=False)
                    ins = pe.matmul(m[:, 0:D], mask[h][:, s], cl[:, jt, :], start=False, stop=off)
                ins.then_inc(unit_done, 1)

            def turn(pair):
                wait(pe, xn_ready, pair + 1)
                wait(pe, xnT_ready, pair)
                for u in range(2):
                    for c in range(DC):
                        s = slice(c * P, (c + 1) * P)
                        ins = pe.transpose(turned[:, u * D + c * P:u * D + (c + 1) * P], xnt[:, u, s],
                                           ident[:, :])
                ins.then_inc(turn_ready, 1)

            def router(pair):
                wait(pe, xnT_ready, pair + 1)
                wait(pe, z_ready, pair)
                if isinstance(pair, int) and pair == 0:
                    pe.wait_ge(small_in, 48)
                for u in range(2):
                    for c in range(DC):
                        ins = pe.matmul(logits[:, u, :], xnT[:, u * D + c * P:u * D + (c + 1) * P],
                                        rw[:, c, :], start=(c == 0), stop=(c == DC - 1))
                ins.then_inc(logits_ready, 1)

            def ranks(pair):
                wait(pe, sel_ready, pair + 1)
                pe.matmul(rank[:, 0, :], tri[:, :], sel[:, 0, :], start=True, stop=True)
                pe.matmul(rank[:, 1, :], tri[:, :], sel[:, 1, :], start=True, stop=False)
                pe.matmul(rank[:, 1, :], ones[:, :], sel[:, 0, :], start=False, stop=True)
                pe.matmul(total, ones[:, :], sel[:, 0, :], start=True, stop=False)
                pe.matmul(total, ones[:, :], sel[:, 1, :], start=False, stop=True).then_inc(rank_ready, 1)

            def body(i):
                unit(i, 0)
                if at_least(i, 2):
                    ranks(i - 2)
                unit(i, 1)
                if at_least(i, 1):
                    turn(i - 1)
                unit(i, 2)
                if at_least(i, 1):
                    router(i - 1)
                unit(i, 3)

            pairs(pe, body)
            ranks(NPAIR - 2)
            turn(NPAIR - 1)
            router(NPAIR - 1)
            ranks(NPAIR - 1)

            def part(e, which, f0, n):
                return W[:, bass.ds(e, 1), which * MATS + f0:which * MATS + f0 + n].rearrange("p a n -> p (a n)")

            def hidden(m, b):
                j = 2 * m + b
                e = pe.value_load(tile_expert[0:1, bass.ds(j, 1)], min_val=0, max_val=E - 1)
                wait(pe, w_in, W_LOADED * e + W_LOADED)
                wait(pe, xs_ready, j + 1)
                for q in range(4):
                    wait(pe, relu_ready, 4 * j + q - 3)
                    for f in range(2 * q, 2 * q + 2):
                        o = h1[q][:, (f % 2) * TT:(f % 2 + 1) * TT]
                        for c in range(DC):
                            x_high, x_low = (xs[b][:, (h * DC + c) * TT:(h * DC + c + 1) * TT]
                                             for h in range(2))
                            w1h, w1l = (part(e, w, c * DFF + f * P, P) for w in (0, 1))
                            pe.matmul(o, w1h, x_high, start=(c == 0), stop=False)
                            pe.matmul(o, w1h, x_low, start=False, stop=False)
                            ins = pe.matmul(o, w1l, x_high, start=False, stop=(c == DC - 1))
                    ins.then_inc(h1_ready, 1)

            def x_turn(m, b):
                j = 2 * m + b
                wait(pe, xg_in[b], 16 * SUB * (m + 1))
                wait(pe, xs_ready, j - 1)
                for h in range(2):
                    for s in range(SUB):
                        for c in range(DC):
                            at = h * DC * TT + c * TT + s * P
                            ins = pe.transpose(xT[b][:, at:at + P],
                                               xg[b][:, s, h * D + c * P:h * D + (c + 1) * P], ident16[:, :])
                ins.then_inc(xt_ready, 1)

            def second(m, b, banks=None):
                j = 2 * m + b
                e = pe.value_load(tile_expert[0:1, bass.ds(j, 1)], min_val=0, max_val=E - 1)
                wait(pe, y_ready, j - 1)
                for s in range(SUB):
                    for f in range(FC):
                        if s == 0 and f % 2 == 0:
                            wait(pe, hl_ready, 4 * j + f // 2 + 1)
                        fs = slice(f * TT + s * P, f * TT + (s + 1) * P)
                        o = (banks[s] if banks else yp[b])[:, s * D:(s + 1) * D]
                        w2h, w2l = (part(e, w, f * D, D) for w in (2, 3))
                        pe.matmul(o, hh[b][:, fs], w2h, start=(f == 0), stop=False)
                        pe.matmul(o, hl[b][:, fs], w2h, start=False, stop=False)
                        ins = pe.matmul(o, hh[b][:, fs], w2l, start=False, stop=(f == FC - 1))
                    if banks or s == SUB - 1:
                        ins.then_inc(yp_ready, 1)

            def step(m, b, more=True):
                hidden(m, b)
                if more:
                    x_turn(*((m, 1) if b == 0 else (m + 1, 0)))
                if not (isinstance(m, int) and 2 * m + b == 0):
                    second(*((m - 1, 1) if b == 0 else (m, 0)))

            pe.wait_ge(tiles_ready, 2)
            pe.wait_ge(listed_in[0], 16)
            warm(10)
            x_turn(0, 0)
            for m in range(2):
                step(m, 0)
                step(m, 1)
            with pe.Fori(2, LAST) as m:
                step(m, 0)
                step(m, 1)
            step(LAST, 0, more=False)
            second(LAST, 0, banks=last_yp)


def kernel(x, adj, L0_ffn_router_w, L0_ffn_w1_all, L0_ffn_b1_all, L0_ffn_w2_all, L0_ffn_b2_all):
    import numpy as np
    import concourse.bacc as bacc
    from concourse.bass_utils import run_bass_kernel_spmd as run

    a = np.asarray
    c = np.ascontiguousarray
    adj_u = c(a(adj).reshape(NPAIR, 2, P, 2, UJ, P).transpose(0, 1, 3, 5, 4, 2)).reshape(NPAIR, 4, P, UNIT)
    w1 = a(L0_ffn_w1_all).reshape(E, DFF, DC, P).transpose(3, 0, 2, 1).reshape(P, E, 1, MATS)
    w2 = a(L0_ffn_w2_all).reshape(E, D, FC, P).transpose(3, 0, 2, 1).reshape(P, E, 1, MATS)
    arrays = {
        "x": c(a(x)),
        "adj_u": adj_u,
        "w_all": c(np.concatenate([w1, w2], axis=2)).reshape(P, E * 2 * MATS),
        "b1_t": c(a(L0_ffn_b1_all).reshape(E, FC, P).transpose(2, 0, 1)).reshape(P, E * FC),
        "b2_r": c(a(L0_ffn_b2_all)).reshape(1, E, D),
        "rw_t": c(a(L0_ffn_router_w).reshape(E, DC, P).transpose(2, 1, 0)),
    }
    nc = bacc.Bacc("TRN2", target_bir_lowering=False, num_devices=1)
    args = {k: nc.dram_tensor(k, v.shape, mybir.dt.from_np(v.dtype), kind="ExternalInput").ap()
            for k, v in arrays.items()}
    out = nc.dram_tensor("out", (N + TT, D), F32, kind="ExternalOutput").ap()
    moe_gnn_kernel(nc, out=out, **args)
    r = run(nc, [arrays], core_ids=[0])
    return r.results[0]["out"][:N]
```
